# Optimizing a Trainium2 kernel written in Bass

```python
import numpy as np
import jax
import jax.numpy as jnp

def _softmax(x, axis=-1):
    return jax.nn.softmax(x, axis=axis)

def _gelu(x):
    return jax.nn.gelu(x, approximate=True)

def _silu(x):
    return jax.nn.silu(x)

def _sigmoid(x):
    return jax.nn.sigmoid(x)

def _layernorm(x, axis=-1, eps=1e-05):
    m = jnp.mean(x, axis=axis, keepdims=True)
    v = jnp.var(x, axis=axis, keepdims=True)
    return (x - m) / jnp.sqrt(v + eps)

def _scatter_add(tgt, idx, src, axis=0):
    return tgt.at[idx].add(src)

def _segment_sum(src, seg, n):
    return jax.ops.segment_sum(src, seg, n)
kernel_name = 'mk_seq_postln_d2_jaxref_r8_8f603c'

def setup_inputs(seed: int=0):
    np.random.seed(seed)
    _w = jnp.asarray

    def _L0_attn_setup():
        import jax, jax.numpy as jnp
        import numpy as np
        B, T, D, H, R = (1, 512, 128, 16, 64)
        HD = D // H
        STD = 0.02

        def _low_rank_proj(x, a, b):
            mid = jnp.einsum('btd,hdr->bhtr', x, a)
            return jnp.einsum('bhtr,hrd->bhtd', mid, b)
        key = jax.random.key(seed)
        ks = jax.random.split(key, 8)
        return {'hidden_states': jax.random.normal(ks[0], (B, T, D), jnp.float32), 'q_a': STD * jax.random.normal(ks[1], (H, D, R), jnp.float32), 'q_b': STD * jax.random.normal(ks[2], (H, R, HD), jnp.float32), 'k_a': STD * jax.random.normal(ks[3], (H, D, R), jnp.float32), 'k_b': STD * jax.random.normal(ks[4], (H, R, HD), jnp.float32), 'v_w': STD * jax.random.normal(ks[5], (D, D), jnp.float32), 'v_b': jnp.zeros((D,), jnp.float32), 'o_w': STD * jax.random.normal(ks[6], (D, D), jnp.float32), 'o_b': jnp.zeros((D,), jnp.float32)}
    _L0_attn_in = _L0_attn_setup()

    def _L0_ffn_setup():
        import jax, jax.numpy as jnp
        import numpy as np
        D_IN, D_HID = (128, 512)

        def _ternary(key, shape):
            return jax.random.randint(key, shape, -1, 2).astype(jnp.float32)

        def _tlin(x, w, s):
            return jnp.einsum('bsi,oi->bso', x, w) * s
        key = jax.random.key(seed)
        ks = jax.random.split(key, 12)
        inv = lambda fan: 1.0 / np.sqrt(fan).astype(np.float32)
        return {'x': jax.random.normal(ks[0], (4, 256, D_IN), dtype=jnp.float32), 'w1_w': _ternary(ks[1], (D_HID, D_IN)), 'w1_s': jax.random.uniform(ks[2], (D_HID,), dtype=jnp.float32) * inv(D_IN), 'w2_w': _ternary(ks[3], (D_HID, D_IN)), 'w2_s': jax.random.uniform(ks[4], (D_HID,), dtype=jnp.float32) * inv(D_IN), 'h1_w': _ternary(ks[5], (D_HID, D_HID)), 'h1_s': jax.random.uniform(ks[6], (D_HID,), dtype=jnp.float32) * inv(D_HID), 'h2_w': _ternary(ks[7], (D_HID, D_HID)), 'h2_s': jax.random.uniform(ks[8], (D_HID,), dtype=jnp.float32) * inv(D_HID), 'w3_w': _ternary(ks[9], (D_IN, D_HID)), 'w3_s': jax.random.uniform(ks[10], (D_IN,), dtype=jnp.float32) * inv(D_HID)}
    _L0_ffn_in = _L0_ffn_setup()

    def _L1_attn_setup():
        import jax, jax.numpy as jnp
        import numpy as np
        from math import sqrt
        EMBED = 128
        HEADS = 16
        key = jax.random.key(seed)
        k1, k2, k3, k4, k5 = jax.random.split(key, 5)
        x = jax.random.normal(k1, (2, 256, EMBED), dtype=jnp.float32)
        s = 1.0 / sqrt(EMBED)
        W_qkv = jax.random.normal(k2, (EMBED, 3 * EMBED), dtype=jnp.float32) * s
        b_qkv = jax.random.normal(k3, (3 * EMBED,), dtype=jnp.float32) * 0.01
        W_out = jax.random.normal(k4, (EMBED, EMBED), dtype=jnp.float32) * s
        b_out = jax.random.normal(k5, (EMBED,), dtype=jnp.float32) * 0.01
        return {'x': x, 'W_qkv': W_qkv, 'b_qkv': b_qkv, 'W_out': W_out, 'b_out': b_out}
    _L1_attn_in = _L1_attn_setup()

    def _L1_ffn_setup():
        import jax, jax.numpy as jnp
        import numpy as np
        B, S, D, F, E, R = (4, 256, 128, 512, 8, 4)
        key = jax.random.key(seed)
        ks = jax.random.split(key, 8)
        s_in = 1.0 / np.sqrt(D)
        s_ff = 1.0 / np.sqrt(F)
        return {'hidden_states': jax.random.normal(ks[0], (B, S, D), jnp.float32), 'gate_W': jax.random.normal(ks[1], (E, D), jnp.float32) * s_in, 'gate_b': jnp.zeros((E,), jnp.float32), 'wi_W': jax.random.normal(ks[2], (F, D), jnp.float32) * s_in, 'wi_b': jnp.zeros((F,), jnp.float32), 'wo_W': jax.random.normal(ks[3], (D, F), jnp.float32) * s_ff, 'wo_b': jnp.zeros((D,), jnp.float32), 'lora_A': jax.random.normal(ks[4], (E, R, D), jnp.float32) * s_in, 'lora_B': jax.random.normal(ks[5], (E, F, R), jnp.float32) * 0.02}
    _L1_ffn_in = _L1_ffn_setup()
    _d = {'L0_attn_hidden_states': _L0_attn_in['hidden_states'], 'L0_attn_q_a': _L0_attn_in['q_a'], 'L0_attn_q_b': _L0_attn_in['q_b'], 'L0_attn_k_a': _L0_attn_in['k_a'], 'L0_attn_k_b': _L0_attn_in['k_b'], 'L0_attn_v_w': _L0_attn_in['v_w'], 'L0_attn_v_b': _L0_attn_in['v_b'], 'L0_attn_o_w': _L0_attn_in['o_w'], 'L0_attn_o_b': _L0_attn_in['o_b'], 'L0_ffn_w1_w': _L0_ffn_in['w1_w'], 'L0_ffn_w1_s': _L0_ffn_in['w1_s'], 'L0_ffn_w2_w': _L0_ffn_in['w2_w'], 'L0_ffn_w2_s': _L0_ffn_in['w2_s'], 'L0_ffn_h1_w': _L0_ffn_in['h1_w'], 'L0_ffn_h1_s': _L0_ffn_in['h1_s'], 'L0_ffn_h2_w': _L0_ffn_in['h2_w'], 'L0_ffn_h2_s': _L0_ffn_in['h2_s'], 'L0_ffn_w3_w': _L0_ffn_in['w3_w'], 'L0_ffn_w3_s': _L0_ffn_in['w3_s'], 'L1_attn_W_qkv': _L1_attn_in['W_qkv'], 'L1_attn_b_qkv': _L1_attn_in['b_qkv'], 'L1_attn_W_out': _L1_attn_in['W_out'], 'L1_attn_b_out': _L1_attn_in['b_out'], 'L1_ffn_gate_W': _L1_ffn_in['gate_W'], 'L1_ffn_gate_b': _L1_ffn_in['gate_b'], 'L1_ffn_wi_W': _L1_ffn_in['wi_W'], 'L1_ffn_wi_b': _L1_ffn_in['wi_b'], 'L1_ffn_wo_W': _L1_ffn_in['wo_W'], 'L1_ffn_wo_b': _L1_ffn_in['wo_b'], 'L1_ffn_lora_A': _L1_ffn_in['lora_A'], 'L1_ffn_lora_B': _L1_ffn_in['lora_B']}
    _x0 = _d['L0_attn_hidden_states']
    _d['L0_attn_hidden_states'] = jax.random.normal(jax.random.fold_in(jax.random.key(seed), 1), (16, 256, 128), dtype=_x0.dtype)
    del _x0
    return _d

def reference(L0_attn_hidden_states, L0_attn_q_a, L0_attn_q_b, L0_attn_k_a, L0_attn_k_b, L0_attn_v_w, L0_attn_v_b, L0_attn_o_w, L0_attn_o_b, L0_ffn_w1_w, L0_ffn_w1_s, L0_ffn_w2_w, L0_ffn_w2_s, L0_ffn_h1_w, L0_ffn_h1_s, L0_ffn_h2_w, L0_ffn_h2_s, L0_ffn_w3_w, L0_ffn_w3_s, L1_attn_W_qkv, L1_attn_b_qkv, L1_attn_W_out, L1_attn_b_out, L1_ffn_gate_W, L1_ffn_gate_b, L1_ffn_wi_W, L1_ffn_wi_b, L1_ffn_wo_W, L1_ffn_wo_b, L1_ffn_lora_A, L1_ffn_lora_B):

    def _L0_attn_ref(hidden_states, q_a, q_b, k_a, k_b, v_w, v_b, o_w, o_b):
        import jax, jax.numpy as jnp
        import numpy as np
        B, T, D, H, R = (1, 512, 128, 16, 64)
        HD = D // H
        STD = 0.02

        def _low_rank_proj(x, a, b):
            mid = jnp.einsum('btd,hdr->bhtr', x, a)
            return jnp.einsum('bhtr,hrd->bhtd', mid, b)
        Bc, Tc, Dc = hidden_states.shape
        q = _low_rank_proj(hidden_states, q_a, q_b)
        k = _low_rank_proj(hidden_states, k_a, k_b)
        v = hidden_states @ v_w.T + v_b
        v = v.reshape(Bc, Tc, H, HD).transpose(0, 2, 1, 3)
        scale = 1.0 / np.sqrt(HD).astype(np.float32)
        att = jnp.einsum('bhtd,bhsd->bhts', q, k) * scale
        causal = jnp.tril(jnp.ones((Tc, Tc), dtype=bool))
        att = jnp.where(causal[None, None], att, jnp.finfo(att.dtype).min)
        att = jax.nn.softmax(att, axis=-1)
        y = jnp.einsum('bhts,bhsd->bhtd', att, v)
        y = y.transpose(0, 2, 1, 3).reshape(Bc, Tc, Dc)
        return y @ o_w.T + o_b

    def _L0_ffn_ref(x, w1_w, w1_s, w2_w, w2_s, h1_w, h1_s, h2_w, h2_s, w3_w, w3_s):
        import jax, jax.numpy as jnp
        import numpy as np
        D_IN, D_HID = (128, 512)

        def _ternary(key, shape):
            return jax.random.randint(key, shape, -1, 2).astype(jnp.float32)

        def _tlin(x, w, s):
            return jnp.einsum('bsi,oi->bso', x, w) * s
        h = jax.nn.silu(_tlin(x, w1_w, w1_s)) * _tlin(x, w2_w, w2_s)
        h = jax.nn.gelu(_tlin(h, h1_w, h1_s), approximate=False)
        h = jax.nn.gelu(_tlin(h, h2_w, h2_s), approximate=False)
        return _tlin(h, w3_w, w3_s)

    def _L1_attn_ref(x, W_qkv, b_qkv, W_out, b_out):
        import jax, jax.numpy as jnp
        import numpy as np
        from math import sqrt
        EMBED = 128
        HEADS = 16
        B, N, E = x.shape
        H = HEADS
        d = E // H
        qkv = x @ W_qkv + b_qkv
        q, k, v = jnp.split(qkv, 3, axis=2)
        q = q.reshape(B, N, H, d)
        k = k.reshape(B, N, H, d)
        v = v.reshape(B, N, H, d)
        energy = jnp.einsum('bqhe,bkhe->bqhk', q, k)
        attn = jax.nn.softmax(energy, axis=-1) / sqrt(E)
        out = jnp.einsum('bihv,bvhd->bihd', attn, v)
        out = out.reshape(B, N, E)
        return out @ W_out + b_out

    def _L1_ffn_ref(hidden_states, gate_W, gate_b, wi_W, wi_b, wo_W, wo_b, lora_A, lora_B):
        import jax, jax.numpy as jnp
        import numpy as np
        B, S, D, F, E, R = (4, 256, 128, 512, 8, 4)
        x = hidden_states
        logits = jnp.einsum('bsd,ed->bse', x, gate_W) + gate_b
        top1 = jnp.argmax(jax.nn.softmax(logits, axis=-1), axis=-1)
        base = jnp.einsum('bsd,fd->bsf', x, wi_W) + wi_b
        out = jnp.zeros_like(x)
        for i in range(lora_A.shape[0]):
            lora = jnp.einsum('bsr,fr->bsf', jnp.einsum('bsd,rd->bsr', x, lora_A[i]), lora_B[i])
            inter = jax.nn.relu(base + lora)
            expert_out = jnp.einsum('bsf,df->bsd', inter, wo_W) + wo_b
            mask = (top1 == i).astype(x.dtype)[..., None]
            out = out + mask * expert_out
        return out
    x = L0_attn_hidden_states
    x = _layernorm(x + _L0_attn_ref(x, L0_attn_q_a, L0_attn_q_b, L0_attn_k_a, L0_attn_k_b, L0_attn_v_w, L0_attn_v_b, L0_attn_o_w, L0_attn_o_b), axis=-1)
    x = _layernorm(x + _L0_ffn_ref(x, L0_ffn_w1_w, L0_ffn_w1_s, L0_ffn_w2_w, L0_ffn_w2_s, L0_ffn_h1_w, L0_ffn_h1_s, L0_ffn_h2_w, L0_ffn_h2_s, L0_ffn_w3_w, L0_ffn_w3_s), axis=-1)
    x = _layernorm(x + _L1_attn_ref(x, L1_attn_W_qkv, L1_attn_b_qkv, L1_attn_W_out, L1_attn_b_out), axis=-1)
    x = _layernorm(x + _L1_ffn_ref(x, L1_ffn_gate_W, L1_ffn_gate_b, L1_ffn_wi_W, L1_ffn_wi_b, L1_ffn_wo_W, L1_ffn_wo_b, L1_ffn_lora_A, L1_ffn_lora_B), axis=-1)
    return x

_drawn_inputs = setup_inputs


def setup_inputs(seed=0):
    import zlib

    import numpy as np

    out = dict(_drawn_inputs(seed))
    spreads = {'L0_attn_v_b': (0.0, 0.356),
     'L0_attn_o_b': (0.0, 0.1),
     'L1_ffn_gate_b': (0.0, 2.0),
     'L1_ffn_wi_b': (0.0, 0.1),
     'L1_ffn_wo_b': (0.0, 0.1)}
    factors = {'L0_attn_q_a': 8.0,
     'L0_attn_q_b': 8.0,
     'L0_attn_k_a': 8.0,
     'L0_attn_k_b': 8.0,
     'L0_attn_v_w': 7.122,
     'L0_ffn_w1_w': 8.0,
     'L0_ffn_w1_s': 8.0,
     'L0_ffn_w2_w': 8.0,
     'L0_ffn_w2_s': 8.0,
     'L0_ffn_h1_w': 8.0,
     'L0_ffn_h1_s': 8.0,
     'L0_ffn_h2_w': 8.0,
     'L0_ffn_h2_s': 8.0,
     'L0_ffn_w3_w': 8.0,
     'L0_ffn_w3_s': 8.0,
     'L1_attn_b_qkv': 55.344,
     'L1_attn_b_out': 5.51,
     'L1_ffn_gate_W': 7.38,
     'L1_ffn_lora_B': 2.674}
    for name, (base, spread) in spreads.items():
        noise = np.random.default_rng([zlib.crc32(name.encode()), seed]).standard_normal(out[name].shape)
        drawn = base * np.exp(spread * noise) if base else spread * noise
        out[name] = jnp.asarray(drawn.astype(out[name].dtype))
    for name, factor in factors.items():
        out[name] = (out[name] * factor).astype(out[name].dtype)
    return out
```

```python
from contextlib import ExitStack

import numpy as np

import concourse.bass as bass
from concourse import mybir

F32 = mybir.dt.float32
BF16 = mybir.dt.bfloat16
ALU = mybir.AluOpType
ACT = mybir.ActivationFunctionType
AX = mybir.AxisListType.X

P = 128
D = 128
HEADS = 16
HD = D // HEADS
SEQ = 256
BATCH = 16
SEQS = 2
TOK = SEQS * SEQ
TILES = TOK // P
CHUNKS = BATCH // SEQS
QB = SEQ // P
GROUP = 4
GROUPS = HEADS // GROUP
PARTS = 3
ROWS = PARTS * PARTS * HD
ROWSM = ROWS + PARTS
HID = 512
HB = HID // P
RANK = 64
EXPERTS = 8
LORA = 4
ER = EXPERTS * LORA
EPS = 1e-5
MASKED = -3.0e38
TWO_ONES = float(np.array([0x3F803F80], np.uint32).view(np.float32)[0])
DMA = 16


COLS = ["w1_s", "w2_s", "h1_s", "h2_s", "wi_b", "q_b", "k_b"]
COL_AT = {n: sum(1 if m in ("q_b", "k_b") else HB for m in COLS[:i]) for i, n in enumerate(COLS)}
NCOLS = COL_AT["k_b"] + 1
ROWS_OF = {"v_b0": D, "o_b0": D, "w3_s": D, "v_b1": D, "o_b1": D, "gate_b": EXPERTS, "wo_b": D}
ROW_AT = {n: sum(list(ROWS_OF.values())[:i]) for i, n in enumerate(ROWS_OF)}
NROW = sum(ROWS_OF.values())

A0, F0, A1, F1 = range(4)


def part_x():
    a, nxt, f = (A1, -1), (A0, 1), (F0, 0)
    return [
        ("pass1", *a, 0, 0), ("merge", A0, 0), ("pass1", *a, 0, 1), ("project", A0, 0), ("norm", A0, 0),
        ("pass1", *a, 0, 2), ("turn", A0, 0), ("pass1", *a, 0, 3), ("maxima", *a, 0),
        ("gated", *f, 0), ("pass1", *a, 1, 0), ("gated", *f, 1), ("pass1", *a, 1, 1), ("gated", *f, 2),
        ("gated", *f, 3),
        ("pass2", *a, 0, 0), ("hidden", *f, 0, 0), ("pass1", *a, 1, 2),
        ("pass2", *a, 0, 1), ("values", *a, 0, 0), ("hidden", *f, 0, 1), ("pass1", *a, 1, 3),
        ("pass2", *a, 0, 2), ("values", *a, 0, 1), ("maxima", *a, 1), ("hidden", *f, 0, 2),
        ("qkv", *nxt), ("pass2", *a, 0, 3), ("values", *a, 0, 2), ("hidden", *f, 0, 3),
        ("pass2", *a, 1, 0), ("values", *a, 0, 3), ("gelu", *f, 0), ("pass2", *a, 1, 1), ("values", *a, 1, 0),
        ("outputs", *a, 0, 0), ("hidden", *f, 1, 0), ("outputs", *a, 0, 1), ("hidden", *f, 1, 1),
        ("pass2", *a, 1, 2), ("values", *a, 1, 1), ("hidden", *f, 1, 2), ("pass2", *a, 1, 3),
        ("values", *a, 1, 2), ("hidden", *f, 1, 3), ("values", *a, 1, 3), ("gelu", *f, 1),
        ("outputs", *a, 1, 0), ("outputs", *a, 1, 1), ("down", *f), ("norm", *f),
    ]


def part_y():
    a, nxt, f = (A0, 1), (A1, 0), (F1, -1)
    return [
        ("pass1", *a, 0, 0), ("merge", A1, -1), ("turn", F0, 0), ("pass1", *a, 0, 1), ("project", A1, -1),
        ("norm", A1, -1), ("pass1", *a, 0, 2), ("turn", A1, -1), ("pass1", *a, 0, 3), ("maxima", *a, 0),
        ("load", A0, 2), ("route", *f), ("pass1", *a, 1, 0), ("pass1", *a, 1, 1), ("lora", *f), ("expert", *f, 0),
        ("pass2", *a, 0, 0), ("pass1", *a, 1, 2), ("expert", *f, 1),
        ("pass2", *a, 0, 1), ("values", *a, 0, 0), ("expert", *f, 2), ("pass1", *a, 1, 3),
        ("pass2", *a, 0, 2), ("values", *a, 0, 1), ("maxima", *a, 1), ("expert", *f, 3),
        ("qkv", *nxt), ("pass2", *a, 0, 3), ("values", *a, 0, 2), ("down", *f), ("norm", *f),
        ("pass2", *a, 1, 0), ("values", *a, 0, 3), ("pass2", *a, 1, 1), ("values", *a, 1, 0),
        ("outputs", *a, 0, 0), ("pass2", *a, 1, 2), ("values", *a, 1, 1), ("outputs", *a, 0, 1),
        ("pass2", *a, 1, 3), ("values", *a, 1, 2), ("store", *f), ("values", *a, 1, 3),
        ("outputs", *a, 1, 0), ("outputs", *a, 1, 1),
    ]


class Last:

    def __init__(self):
        self.c, self.of = 0, {}

    def next_chunk(self, c):
        self.c = c
        self.of = {key: (s, per, dn - 1, k) for key, (s, per, dn, k) in self.of.items()}

    def used(self, key, sem, per, dn, k):
        self.of[key] = (sem, per, dn, k)

    def wait(self, engine, key):
        if key in self.of:
            sem, per, dn, k = self.of[key]
            engine.wait_ge(sem, per * (self.c + dn) + k)


def walk(engine, steps, last=None):

    def chunk(c, present):
        if last:
            last.next_chunk(c)
        for name, stage, dn, *args in part_x() + part_y():
            if name in steps and present(dn):
                steps[name](stage, dn, c + dn, *args)

    for c in range(-2, 2):
        chunk(c, lambda dn: 0 <= c + dn < CHUNKS)
    before = dict(last.of) if last else None
    with engine.Fori(2, CHUNKS - 2) as c:
        chunk(c, lambda dn: True)
        assert not last or before == last.of, (before, last.of)
    for c in range(CHUNKS - 2, CHUNKS + 1):
        chunk(c, lambda dn: 0 <= c + dn < CHUNKS)


def build(nc, d_in, out):
    ctx = ExitStack()
    with ctx:
        def sb(name, shape, dt=F32):
            return ctx.enter_context(nc.sbuf_tensor(name, shape, dt))

        def ps(name, shape):
            return ctx.enter_context(nc.psum_tensor(name, shape, F32))

        def sem(name):
            return ctx.enter_context(nc.semaphore(name))

        ps_s1 = ps("ps_s1", [P, 2, 512])
        ps_s2 = ps("ps_s2", [P, 2, 512])
        ps_o = ps("ps_o", [P, 512])
        ps_m = ps("ps_m", [P, 512])
        ps_f = ps("ps_f", [P, 2, 512])

        wqb = sb("wqb", [RANK, HEADS, 2, HD])
        wq = {s: sb(f"wq{s}", [P, 2, D]) for s in (A0, A1)}
        wv = {s: sb(f"wv{s}", [P, D]) for s in (A0, A1)}
        wo = {s: sb(f"wo{s}", [P, D]) for s in (A0, A1)}
        w12 = sb("w12", [P, 2, HID])
        wh = sb("wh", [P, 2, HB, HID])
        w3 = sb("w3", [P, HB, D])
        wi = sb("wi", [P, HID])
        wgl = sb("wgl", [P, EXPERTS + ER])
        wlb = sb("wlb", [ER, HID])
        wout = sb("wout", [P, HB, D])
        cols = sb("cols", [P, NCOLS])
        rows = sb("rows", [P, NROW])
        half_s = sb("half_s", [P, HB])
        gate_s = sb("gate_s", [P, HB])
        ident = sb("ident", [P, P])
        identb = sb("identb", [P, P], BF16)
        above = sb("above", [P, P], BF16)
        ranks = sb("ranks", [P, EXPERTS])
        minus_half = sb("minus_half", [P, TILES])
        dve_carrier = sb("dve_carrier", [P, 4])
        pool_carrier = sb("pool_carrier", [P, SEQS * GROUPS])

        def col(name, i=0):
            return cols[:, COL_AT[name] + i:COL_AT[name] + i + 1]

        def row(name):
            return rows[:, ROW_AT[name]:ROW_AT[name] + ROWS_OF[name]]

        x = {s: sb(f"x{s}", [P, TILES, D]) for s in (A0, F0, A1, F1)}
        x["out"] = sb("xout", [P, TILES, D])
        xt = {s: sb(f"xt{s}", [P, TOK]) for s in (A0, F0, A1, F1)}
        resid = {s: sb(f"resid{s}", [P, TILES, D]) for s in (A0, A1, F1)}
        resid[F0] = x[F0]
        into = {A0: F0, F0: A1, A1: F1, F1: "out"}
        ln_sum = sb("ln_sum", [P, TILES, D])
        ln_parts = sb("ln_parts", [P, TILES, 6])
        ln_stat = {s: sb(f"ln_stat{s}", [P, TILES, 2]) for s in range(4)}
        ln_var = {s: sb(f"ln_var{s}", [P, TILES]) for s in range(4)}
        ln_rstd = {s: sb(f"ln_rstd{s}", [P, TILES]) for s in range(4)}

        split = sb("split", [P, 2, PARTS, TOK], BF16)
        rest = sb("rest", [P, 2, TOK])
        qrow = {s: sb(f"qrow{s}", [P, HEADS, TOK], BF16) for s in (A0, A1)}
        krow = {s: sb(f"krow{s}", [P, HEADS, TOK], BF16) for s in (A0, A1)}
        v = {s: sb(f"v{s}", [P, TILES, HEADS, 32]) for s in (A0, A1)}
        top = {s: sb(f"top{s}", [P, SEQS, QB, HEADS]) for s in (A0, A1)}
        tsplit = sb("tsplit", [HEADS, SEQS, PARTS, SEQ], BF16)
        trest = sb("trest", [HEADS, SEQ])
        prob = sb("prob", [P, 2, GROUP, QB * SEQ])
        osum = sb("osum", [P, SEQS, GROUPS, SEQ])
        recip = sb("recip", [P, HEADS])
        y = sb("y", [P, TILES, D])
        yt = sb("yt", [P, TOK])

        hid = sb("hid", [P, HB, TOK])
        gel = sb("gel", [P, HB, TOK])
        hidden_of = (gel, hid)
        wqa = prob[0:RANK].rearrange("p a g t -> p (a g t)").rearrange("p (h s d) -> p h s d", h=HEADS, s=2)
        w3raw = gel[:, 0, :].rearrange("p (k d) -> p k d", k=HB)
        logit = sb("logit", [P, TILES, EXPERTS])
        best = sb("best", [P, TILES])
        pick = sb("pick", [P, TILES, EXPERTS])
        first = sb("first", [P, TILES])
        low = sb("low", [P, TILES, ER])
        lowt = sb("lowt", [ER, TOK])

        weights = sem("weights")
        weights0 = sem("weights0")
        made = sem("made")
        folded = sem("folded")
        wready = sem("wready")
        loaded = sem("loaded")
        stored = sem("stored")

        def per_stage(name, stages=(A0, A1)):
            return {s: sem(f"{name}{s}") for s in stages}

        proj_full = per_stage("proj_full")
        part1 = per_stage("part1")
        parts = per_stage("parts")
        v_done = per_stage("v_done")
        spread = per_stage("spread")
        s1_full = per_stage("s1_full")
        maxed = per_stage("maxed")
        top_full = per_stage("top_full")
        tparts = per_stage("tparts")
        trows = per_stage("trows")
        s2_full = per_stage("s2_full")
        exped = per_stage("exped")
        causal = sem("causal")
        pv_full = per_stage("pv_full")
        o_done = per_stage("o_done")
        ot_full = per_stage("ot_full")
        scaled = per_stage("scaled")
        yt_full = per_stage("yt_full")
        yt_done = per_stage("yt_done")
        out_full = per_stage("out_full", range(4))
        ln = per_stage("ln", range(4))
        rstd = per_stage("rstd", range(4))
        biased = per_stage("biased", (A0, A1, F1))
        xt_full = per_stage("xt_full", range(3))
        xt_done = per_stage("xt_done", range(3))
        gate_full = sem("gate_full")
        tanhed = sem("tanhed")
        gated = sem("gated")
        hid_full = sem("hid_full")
        hid_done = sem("hid_done")
        gelued = sem("gelued")
        route_full = sem("route_full")
        routed = sem("routed")
        lora_full = sem("lora_full")
        lora_done = sem("lora_done")
        exp_full = sem("exp_full")
        relued = sem("relued")

        S1 = {A0: SEQS * GROUPS * 3, A1: SEQS * GROUPS * 4}
        NSPREAD = 2 * PARTS * PARTS * DMA
        S2 = SEQS * HEADS
        NWEIGHTS = 14 * DMA

        block = ctx.enter_context(nc.Block())

        @block.sync
        def _(sp):
            sp.dma_start(wqa, d_in["qk_a"]).then_inc(weights0, DMA)
            sp.dma_start(wqb[:], d_in["qk_b"]).then_inc(weights0, DMA)

            def load(s, dn, n):
                if not isinstance(n, int) or n:
                    sp.wait_ge(proj_full[A0], 3 * n)
                    sp.wait_ge(biased[A0], 1 * n)
                sp.dma_start(xt[A0][:], d_in["xt"][:, bass.ts(n, TOK)]).then_inc(loaded, DMA)
                sp.dma_start(x[A0][:], d_in["x"][bass.ts(n, TOK), :].rearrange("(t p) d -> p t d", p=P)).then_inc(loaded, DMA)

            def qkv(s, dn, n):
                for side, dst in ((0, qrow[s]), (1, krow[s])):
                    sp.wait_ge(parts[s], 6 * n + 3 * side + 3)
                    for i in range(PARTS):
                        for j in range(PARTS):
                            r = (i * PARTS + j) * HD
                            src = split[:, side, (i, j)[side], :]
                            sp.dma_start(dst[r:r + HD, :, :], src).then_inc(spread[s], DMA)

            def maxima(s, dn, n, b):
                sp.wait_ge(tparts[s], 8 * n + 4 * b + 4)
                for i in range(PARTS):
                    sp.dma_start(qrow[s][ROWS + i:ROWS + i + 1, :, b * SEQ:(b + 1) * SEQ],
                                 tsplit[:, b, i, :]).then_inc(trows[s], DMA)

            def store(s, dn, n):
                sp.wait_ge(ln[F1], 5 * n + 5)
                sp.dma_start(out[bass.ts(n, TOK), :].rearrange("(t p) d -> p t d", p=P), x["out"][:]).then_inc(stored, DMA)

            walk(sp, dict(load=load, qkv=qkv, maxima=maxima, store=store))
            sp.wait_ge(stored, CHUNKS * DMA)

        @block.gpsimd
        def _(pool):
            nc.gpsimd.memset(ident[:], 0.0)
            nc.gpsimd.memset(above[:], 0.0)
            nc.gpsimd.memset(minus_half[:], -0.5)
            nc.gpsimd.iota(ranks[:], pattern=[[1, EXPERTS]], base=-EXPERTS, channel_multiplier=0,
                           allow_small_or_imprecise_dtypes=True)
            for s in (A0, A1):
                nc.gpsimd.memset(v[s][:].rearrange("p t h c -> p (t h c)"), 1.0 if s == A0 else float(np.sqrt(D)))
            nc.gpsimd.memset(identb[:], 0.0).then_inc(made, 1)
            pool.wait_ge(made, 1)
            nc.gpsimd.affine_select(out=ident[:], in_=ident[:], compare_op=ALU.not_equal, fill=1.0,
                                    base=0, pattern=[[-1, P]], channel_multiplier=1)
            nc.gpsimd.affine_select(out=identb[:], in_=identb[:], compare_op=ALU.not_equal, fill=1.0,
                                    base=0, pattern=[[-1, P]], channel_multiplier=1)
            nc.gpsimd.affine_select(out=above[:], in_=above[:], compare_op=ALU.is_ge, fill=MASKED,
                                    base=0, pattern=[[-1, P]], channel_multiplier=1).then_inc(made, 1)
            pool.wait_ge(weights, NWEIGHTS)

            def residual(s, n, bias):
                nc.gpsimd.tensor_tensor(resid[s][:], x[s][:], row(bias).unsqueeze(1).to_broadcast([P, TILES, D]),
                                        ALU.add).then_inc(biased[s], 1)

            def qkv(s, dn, n):
                if s == A0:
                    pool.wait_ge(loaded, 2 * DMA * n + 2 * DMA)
                else:
                    pool.wait_ge(ln[F0], 5 * n + 5)
                if not isinstance(n, int) or n:
                    pool.wait_ge(ln[s], 5 * n - 4)
                residual(s, n, "o_b0" if s == A0 else "o_b1")

            def route(s, dn, n):
                pool.wait_ge(ln[A1], 5 * n + 5)
                if not isinstance(n, int) or n:
                    pool.wait_ge(ln[F1], 5 * n - 4)
                residual(F1, n, "wo_b")

            def norm(s, dn, n):
                pool.wait_ge(ln[s], 5 * n + 4)
                nc.gpsimd.tensor_tensor(ln_rstd[s][:], ln_var[s][:], minus_half[:], ALU.pow).then_inc(rstd[s], 1)

            def pass2(s, dn, n, b, j):
                if s == A0:
                    pool.wait_ge(exped[A0], S2 * n + HEADS * b + GROUP * (j + 1))
                    k = GROUPS * b + j
                    nc.gpsimd.tensor_tensor(pool_carrier[:, k:k + 1], minus_half[:, 0:1], minus_half[:, 0:1], ALU.add)
                    diag = prob[:, j % 2].rearrange("p h (k q) -> p h k q", k=2)[:, :, :, 0:P]
                    nc.gpsimd.affine_select(out=diag, in_=diag, compare_op=ALU.is_ge, fill=0.0, base=0,
                                            pattern=[[0, GROUP], [0, QB], [1, P]],
                                            channel_multiplier=-1).then_inc(causal, 1)

            walk(pool, dict(qkv=qkv, route=route, norm=norm, pass2=pass2))

        @block.scalar
        def _(act):
            for dst, name in ((wv[A0][:], "v_w0"), (wo[A0][:], "o_w0"), (cols[:], "cols"), (w12[:], "w12"),
                              (wh[:], "wh"), (w3raw, "w3"), (wq[A1][:], "qk_w1"), (wv[A1][:], "v_w1"),
                              (wo[A1][:], "o_w1"), (wi[:], "wi"), (wgl[:], "gl"), (wlb[:], "lb"), (wout[:], "wo")):
                act.dma_start(dst, d_in[name]).then_inc(weights, DMA)
            act.dma_start(rows[:], d_in["rows"].partition_broadcast(P)).then_inc(weights, DMA)
            act.wait_ge(wready, 5)
            last = Last()

            def qkv(s, dn, n):
                for side, bias in ((0, "q_b"), (1, "k_b")):
                    act.wait_ge(proj_full[s], 3 * n + side + 1)
                    nc.scalar.activation(split[:, side, 0, :], ps_m[:], ACT.Identity,
                                         bias=0.0 if s == A0 else col(bias)).then_inc(part1[s], 1)

            def pass2(s, dn, n, b, j):
                wide = SEQ + P if s == A0 else QB * SEQ
                last.wait(act, ("prob", j % 2))
                for g in range(GROUP):
                    k = HEADS * b + GROUP * j + g
                    act.wait_ge(s2_full[s], S2 * n + k + 1)
                    nc.scalar.activation(prob[:, j % 2, g, 0:wide], ps_s2[:, g % 2, 0:wide], ACT.Exp,
                                         scale=1.0 / float(np.sqrt(np.float32(HD))) if s == A0 else 1.0).then_inc(exped[s], 1)
                last.used(("prob", j % 2), pv_full[s], SEQS * GROUPS, dn, GROUPS * b + j + 1)

            def values(s, dn, n, b, j):
                act.wait_ge(pv_full[s], SEQS * GROUPS * n + GROUPS * b + j + 1)
                nc.scalar.activation(osum[:, b, j, :], ps_o[:, 0:SEQ], ACT.Copy).then_inc(o_done[s], 1)

            def merge(s, dn, n):
                act.wait_ge(yt_full[s], 1 * n + 1)
                nc.scalar.activation(yt[:], ps_m[:], ACT.Copy).then_inc(yt_done[s], 1)

            def turn(s, dn, n):
                act.wait_ge(xt_full[s], 1 * n + 1)
                src = ps_f[:, 1, :] if s == F0 else ps_m[:]
                nc.scalar.activation(xt[into[s]][:], src, ACT.Copy).then_inc(xt_done[s], 1)

            def gated_(s, dn, n, m):
                act.wait_ge(gate_full, 2 * HB * n + 2 * m + 1)
                nc.scalar.activation(hid[:, m, :], ps_f[:, 0, :], ACT.Tanh, scale=half_s[:, m:m + 1]).then_inc(tanhed, 1)

            def gelu(s, dn, n, layer):
                act.wait_ge(hid_done, 2 * HB * n + HB * (layer + 1))
                nc.scalar.activation(hidden_of[layer][:], hidden_of[layer][:], ACT.Gelu).then_inc(gelued, 1)

            def lora(s, dn, n):
                act.wait_ge(lora_full, 1 * n + 1)
                nc.scalar.activation(lowt[:], ps_f[0:ER, 1, :], ACT.Copy).then_inc(lora_done, 1)

            def expert(s, dn, n, m):
                act.wait_ge(exp_full, HB * n + m + 1)
                nc.scalar.activation(hid[:, m, :], ps_f[:, m % 2, :], ACT.Relu, bias=col("wi_b", m)).then_inc(relued, 1)

            walk(act, dict(qkv=qkv, pass2=pass2, values=values, merge=merge, turn=turn, gated=gated_, gelu=gelu,
                           lora=lora, expert=expert), last)

        @block.vector
        def _(dve):
            for s in (A0, A1):
                nc.vector.memset(krow[s][64:96, :, :].rearrange("p h t -> p (h t)").bitcast(F32), TWO_ONES)
            dve.wait_ge(folded, 1)
            nc.vector.tensor_copy(wq[A0][:].rearrange("p a c -> p (a c)"), ps_m[:, 0:2 * D]).then_inc(wready, 1)
            dve.wait_ge(weights, NWEIGHTS)
            nc.vector.tensor_scalar(half_s[:], cols[:, COL_AT["w1_s"]:COL_AT["w1_s"] + HB], 0.5, None, ALU.mult).then_inc(wready, 1)
            dve.wait_ge(wready, 2)
            nc.vector.tensor_tensor(gate_s[:], half_s[:], cols[:, COL_AT["w2_s"]:COL_AT["w2_s"] + HB], ALU.mult).then_inc(wready, 1)
            nc.vector.tensor_tensor(w3[:], w3raw, row("w3_s").unsqueeze(1).to_broadcast([P, HB, D]), ALU.mult).then_inc(wready, 1)
            dve.wait_ge(made, 2)
            nc.vector.memset(recip[:], 0.0).then_inc(wready, 1)

            def qkv(s, dn, n):
                for side, bias in ((0, "q_b"), (1, "k_b")):
                    r = rest[:, side, :]
                    dve.wait_ge(part1[s], 2 * n + side + 1)
                    nc.vector.scalar_tensor_tensor(out=r, in0=ps_m[:], scalar=0.0 if s == A0 else col(bias),
                                                   in1=split[:, side, 0, :], op0=ALU.add,
                                                   op1=ALU.subtract).then_inc(parts[s], 1)
                    dve.wait_ge(parts[s], 6 * n + 3 * side + 1)
                    nc.vector.tensor_copy(split[:, side, 1, :], r).then_inc(parts[s], 1)
                    dve.wait_ge(parts[s], 6 * n + 3 * side + 2)
                    nc.vector.tensor_tensor(split[:, side, 2, :], r, split[:, side, 1, :],
                                            ALU.subtract).then_inc(parts[s], 1)
                dve.wait_ge(proj_full[s], 3 * n + 3)
                bias = row("v_b0" if s == A0 else "v_b1").rearrange("p (h c) -> p h c", c=HD)
                for t in range(TILES):
                    done = nc.vector.tensor_tensor(v[s][:, t, :, 0:HD], ps_m[:, t * D:(t + 1) * D].rearrange("p (h c) -> p h c", c=HD),
                                                   bias, ALU.add)
                done.then_inc(v_done[s], 1)

            def pass1(s, dn, n, b, j):
                units = S1[s] // (SEQS * GROUPS)
                for u in range(units):
                    k = (GROUPS * b + j) * units + u
                    dve.wait_ge(s1_full[s], S1[s] * n + k + 1)
                    bank = ps_s1[:, k % 2, :]
                    h = GROUP * j
                    if s == A0 and u == 0:
                        dst, src = top[s][:, b, 0, h:h + 4], bank.rearrange("p (h k) -> p h k", h=4)
                    else:
                        qb, pair = (1, u - 1) if s == A0 else (u % 2, u // 2)
                        dst = top[s][:, b, qb, h + 2 * pair:h + 2 * pair + 2]
                        src = bank.rearrange("p (h k) -> p h k", h=2)
                    nc.vector.tensor_reduce(out=dst, in_=src, axis=AX, op=ALU.max, negate=True).then_inc(maxed[s], 1)

            def maxima(s, dn, n, b):
                src = ps_m[0:HEADS, 0:SEQ]
                t = tsplit[:, b]
                dve.wait_ge(top_full[s], 2 * n + b + 1)
                nc.vector.tensor_copy(t[:, 0, :], src).then_inc(tparts[s], 1)
                dve.wait_ge(tparts[s], 8 * n + 4 * b + 1)
                nc.vector.tensor_tensor(trest[:], src, t[:, 0, :], ALU.subtract).then_inc(tparts[s], 1)
                dve.wait_ge(tparts[s], 8 * n + 4 * b + 2)
                nc.vector.tensor_copy(t[:, 1, :], trest[:]).then_inc(tparts[s], 1)
                dve.wait_ge(tparts[s], 8 * n + 4 * b + 3)
                nc.vector.tensor_tensor(t[:, 2, :], trest[:], t[:, 1, :], ALU.subtract).then_inc(tparts[s], 1)

            def outputs(s, dn, n, b, qb):
                i = QB * b + qb
                src = ps_m[:].rearrange("p (h c) -> p h c", c=32)
                dve.wait_ge(ot_full[s], 4 * n + i + 1)
                nc.vector.reciprocal(recip[:], src[:, :, HD]).then_inc(scaled[s], 1)
                dve.wait_ge(scaled[s], 8 * n + 2 * i + 1)
                nc.vector.tensor_tensor(y[:, i, :].rearrange("p (h c) -> p h c", c=HD), src[:, :, 0:HD],
                                        recip[:].unsqueeze(2).to_broadcast([P, HEADS, HD]),
                                        ALU.mult).then_inc(scaled[s], 1)

            def norm(s, dn, n):
                src = ps_m[:] if s in (A0, A1) else ps_f[:, 0, :]
                dve.wait_ge(out_full[s], 1 * n + 1)
                if s == F0:
                    dve.wait_ge(ln[A0], 5 * n + 5)
                else:
                    dve.wait_ge(biased[s], 1 * n + 1)
                nc.vector.tensor_tensor(ln_sum[:], src.rearrange("p (t d) -> p t d", t=TILES), resid[s][:],
                                        ALU.add).then_inc(ln[s], 1)
                dve.wait_ge(ln[s], 5 * n + 1)
                for t in range(TILES):
                    done = nc.vector.bn_stats(ln_parts[:, t, :], ln_sum[:, t, :])
                done.then_inc(ln[s], 1)
                dve.wait_ge(ln[s], 5 * n + 2)
                nc.vector.memset(dve_carrier[:, s:s + 1], 0.0)
                for t in range(TILES):
                    done = nc.vector.bn_aggr(ln_stat[s][:, t, :], ln_parts[:, t, :])
                done.then_inc(ln[s], 1)
                dve.wait_ge(ln[s], 5 * n + 3)
                nc.vector.tensor_scalar(ln_var[s][:], ln_stat[s][:, :, 1], EPS, None, ALU.add).then_inc(ln[s], 1)
                dve.wait_ge(rstd[s], 1 * n + 1)
                if s == F1 and (not isinstance(n, int) or n):
                    dve.wait_ge(stored, DMA * n)
                for t in range(TILES):
                    done = nc.vector.tensor_scalar(x[into[s]][:, t, :], ln_sum[:, t, :], ln_stat[s][:, t, 0:1],
                                                   ln_rstd[s][:, t:t + 1], ALU.subtract, ALU.mult)
                done.then_inc(ln[s], 1)

            def gated_(s, dn, n, m):
                dve.wait_ge(tanhed, HB * n + m + 1)
                nc.vector.scalar_tensor_tensor(out=hid[:, m, :], in0=hid[:, m, :], scalar=1.0, in1=ps_f[:, 0, :],
                                               op0=ALU.add, op1=ALU.mult).then_inc(gated, 1)
                dve.wait_ge(gate_full, 2 * HB * n + 2 * m + 2)
                dve.wait_ge(gated, 2 * HB * n + 2 * m + 1)
                nc.vector.scalar_tensor_tensor(out=hid[:, m, :], in0=ps_f[:, 1, :], scalar=gate_s[:, m:m + 1],
                                               in1=hid[:, m, :], op0=ALU.mult, op1=ALU.mult).then_inc(gated, 1)

            def hidden(s, dn, n, layer, m):
                dve.wait_ge(hid_full, 2 * HB * n + HB * layer + m + 1)
                nc.vector.tensor_scalar(hidden_of[layer][:, m, :], ps_f[:, m % 2, :], col(("h1_s", "h2_s")[layer], m), None,
                                        ALU.mult).then_inc(hid_done, 1)

            def route(s, dn, n):
                src = ps_f[:, 0, 0:TILES * (EXPERTS + ER)].rearrange("p (t c) -> p t c", t=TILES)
                wide = [P, TILES, EXPERTS]

                def step(k, ins):
                    ins.then_inc(routed, 1)
                    dve.wait_ge(routed, 7 * n + k)

                dve.wait_ge(route_full, 1 * n + 1)
                step(1, nc.vector.tensor_tensor(logit[:], src[:, :, 0:EXPERTS], row("gate_b").unsqueeze(1).to_broadcast(wide), ALU.add))
                step(2, nc.vector.tensor_reduce(out=best[:], in_=logit[:], axis=AX, op=ALU.max))
                step(3, nc.vector.tensor_tensor(pick[:], logit[:], best[:].unsqueeze(2).to_broadcast(wide), ALU.is_ge))
                step(4, nc.vector.tensor_tensor(pick[:], pick[:], ranks[:].unsqueeze(1).to_broadcast(wide), ALU.mult))
                step(5, nc.vector.tensor_reduce(out=first[:], in_=pick[:], axis=AX, op=ALU.min))
                step(6, nc.vector.tensor_tensor(pick[:], pick[:], first[:].unsqueeze(2).to_broadcast(wide), ALU.is_equal))
                nc.vector.tensor_tensor(low[:].rearrange("p t (e r) -> p t e r", r=LORA),
                                        src[:, :, EXPERTS:].rearrange("p t (e r) -> p t e r", r=LORA),
                                        pick[:].unsqueeze(3).to_broadcast([P, TILES, EXPERTS, LORA]),
                                        ALU.mult).then_inc(routed, 1)

            walk(dve, dict(qkv=qkv, pass1=pass1, maxima=maxima, outputs=outputs, norm=norm, gated=gated_,
                           hidden=hidden, route=route))

        @block.tensor
        def _(pe):
            pe.wait_ge(weights0, 2 * DMA)
            for side in range(2):
                for h in range(HEADS):
                    at = ps_m[:, side * D:(side + 1) * D].rearrange("p (c h) -> p c h", h=HEADS)[:, :, h]
                    done = nc.tensor.matmul(at, wqa[:, h, side, :], wqb[:, h, side, :], start=True, stop=True)
            done.then_inc(folded, 1)
            pe.wait_ge(wready, 5)
            last = Last()

            def qkv(s, dn, n):
                if s == A0:
                    pe.wait_ge(loaded, 2 * DMA * n + 2 * DMA)
                else:
                    pe.wait_ge(xt_done[F0], 1 * n + 1)
                for side in range(2):
                    last.wait(pe, "m")
                    nc.tensor.matmul(ps_m[:], wq[s][:, side, :], xt[s][:], start=True, stop=True).then_inc(proj_full[s], 1)
                    last.used("m", parts[s], 6, dn, 3 * side + 1)
                last.wait(pe, "m")
                for t in range(TILES):
                    done = nc.tensor.matmul(ps_m[:, t * D:(t + 1) * D], xt[s][:, t * P:(t + 1) * P], wv[s][:],
                                            start=True, stop=True)
                done.then_inc(proj_full[s], 1)
                last.used("m", v_done[s], 1, dn, 1)

            def pass1(s, dn, n, b, j):
                if b == 0 and j == 0:
                    pe.wait_ge(spread[s], NSPREAD * n + NSPREAD)
                units = S1[s] // (SEQS * GROUPS)

                def keys(h, blocks):
                    return krow[s][0:ROWS, h, b * SEQ:b * SEQ + blocks * P]

                def queries(h, qb):
                    return qrow[s][0:ROWS, h, b * SEQ + qb * P:b * SEQ + (qb + 1) * P]

                def mask(at):
                    return nc.tensor.matmul(at, identb[:], above[:], start=False, stop=True, skip_group_check=True)

                for u in range(units):
                    k = (GROUPS * b + j) * units + u
                    bank = ps_s1[:, k % 2, :]
                    last.wait(pe, ("s1", k % 2))
                    if s == A0 and u == 0:
                        for g in range(GROUP):
                            at = bank[:, g * P:(g + 1) * P]
                            nc.tensor.matmul(at, queries(GROUP * j + g, 0), keys(GROUP * j + g, 1), start=True, stop=False,
                                             skip_group_check=True)
                            done = mask(at)
                    else:
                        qb, pair = (1, u - 1) if s == A0 else (u % 2, u // 2)
                        for g in range(2):
                            h = GROUP * j + 2 * pair + g
                            at = bank[:, g * SEQ:(g + 1) * SEQ]
                            done = nc.tensor.matmul(at, queries(h, qb), keys(h, 2), start=True, stop=s == A1,
                                                    skip_group_check=True)
                            if s == A0:
                                done = mask(at[:, P:])
                    done.then_inc(s1_full[s], 1)
                    last.used(("s1", k % 2), maxed[s], S1[s], dn, k + 1)

            def maxima(s, dn, n, b):
                pe.wait_ge(maxed[s], S1[s] * n + S1[s] // SEQS * (b + 1))
                last.wait(pe, "m")
                for qb in range(QB):
                    done = nc.tensor.transpose(ps_m[0:HEADS, qb * P:(qb + 1) * P], top[s][:, b, qb, :], ident[:])
                done.then_inc(top_full[s], 1)
                last.used("m", tparts[s], 8, dn, 4 * b + 2)

            def pass2(s, dn, n, b, j):
                if j == 0:
                    pe.wait_ge(trows[s], 2 * PARTS * DMA * n + PARTS * DMA * (b + 1))
                for g in range(GROUP):
                    h = GROUP * j + g
                    bank = ps_s2[:, g % 2, :]
                    last.wait(pe, ("s2", g % 2))
                    for kb in range(QB):
                        q0 = P * kb if s == A0 else 0
                        done = nc.tensor.matmul(bank[:, kb * SEQ:(kb + 1) * SEQ - q0],
                                                krow[s][0:ROWSM, h, b * SEQ + kb * P:b * SEQ + (kb + 1) * P],
                                                qrow[s][0:ROWSM, h, b * SEQ + q0:(b + 1) * SEQ], start=True, stop=True)
                    done.then_inc(s2_full[s], 1)
                    last.used(("s2", g % 2), exped[s], S2, dn, HEADS * b + h + 1)

            def values(s, dn, n, b, j):
                if s == A0:
                    pe.wait_ge(causal, SEQS * GROUPS * n + GROUPS * b + j + 1)
                else:
                    pe.wait_ge(exped[s], S2 * n + HEADS * b + GROUP * (j + 1))
                if b == 0 and j == 0:
                    pe.wait_ge(v_done[s], 1 * n + 1)
                last.wait(pe, "o")
                for kb in range(QB):
                    q0 = P * kb if s == A0 else 0
                    for g in range(GROUP):
                        done = nc.tensor.matmul(ps_o[32 * g:32 * g + 32, q0:SEQ], v[s][:, QB * b + kb, GROUP * j + g, :],
                                                prob[:, j % 2, g, kb * SEQ:(kb + 1) * SEQ - q0],
                                                start=kb == 0, stop=kb == QB - 1, skip_group_check=True)
                done.then_inc(pv_full[s], 1)
                last.used("o", o_done[s], SEQS * GROUPS, dn, GROUPS * b + j + 1)

            def outputs(s, dn, n, b, qb):
                if qb == 0:
                    pe.wait_ge(o_done[s], SEQS * GROUPS * n + GROUPS * (b + 1))
                last.wait(pe, "m")
                for j in range(GROUPS):
                    done = nc.tensor.transpose(ps_m[:, j * P:(j + 1) * P], osum[:, b, j, qb * P:(qb + 1) * P], ident[:])
                done.then_inc(ot_full[s], 1)
                last.used("m", scaled[s], 8, dn, 2 * (QB * b + qb) + 2)

            def merge(s, dn, n):
                pe.wait_ge(scaled[s], 8 * n + 8)
                last.wait(pe, "m")
                for t in range(TILES):
                    done = nc.tensor.transpose(ps_m[:, t * P:(t + 1) * P], y[:, t, :], ident[:])
                done.then_inc(yt_full[s], 1)
                last.used("m", yt_done[s], 1, dn, 1)

            def project(s, dn, n):
                pe.wait_ge(yt_done[s], 1 * n + 1)
                last.wait(pe, "m")
                for t in range(TILES):
                    done = nc.tensor.matmul(ps_m[:, t * D:(t + 1) * D], yt[:, t * P:(t + 1) * P], wo[s][:],
                                            start=True, stop=True)
                done.then_inc(out_full[s], 1)
                last.used("m", ln[s], 5, dn, 1)

            def turn(s, dn, n):
                key, bank = (("f", 1), ps_f[:, 1, :]) if s == F0 else ("m", ps_m[:])
                pe.wait_ge(ln[s], 5 * n + 5)
                last.wait(pe, key)
                for t in range(TILES):
                    done = nc.tensor.transpose(bank[:, t * P:(t + 1) * P], x[into[s]][:, t, :], ident[:])
                done.then_inc(xt_full[s], 1)
                last.used(key, xt_done[s], 1, dn, 1)

            def gated_(s, dn, n, m):
                if m == 0:
                    pe.wait_ge(xt_done[A0], 1 * n + 1)
                for side in range(2):
                    last.wait(pe, ("f", side))
                    nc.tensor.matmul(ps_f[:, side, :], w12[:, side, m * P:(m + 1) * P], xt[F0][:], start=True,
                                     stop=True).then_inc(gate_full, 1)
                    last.used(("f", side), gated, 2 * HB, dn, 2 * m + 1 + side)

            def hidden(s, dn, n, layer, m):
                if m == 0:
                    if layer == 0:
                        pe.wait_ge(gated, 2 * HB * n + 2 * HB)
                    else:
                        pe.wait_ge(gelued, 2 * n + 1)
                last.wait(pe, ("f", m % 2))
                src = (hid, gel)[layer]
                for k in range(HB):
                    done = nc.tensor.matmul(ps_f[:, m % 2, :], wh[:, layer, k, m * P:(m + 1) * P], src[:, k, :],
                                            start=k == 0, stop=k == HB - 1)
                done.then_inc(hid_full, 1)
                last.used(("f", m % 2), hid_done, 2 * HB, dn, HB * layer + m + 1)

            def route(s, dn, n):
                pe.wait_ge(xt_done[A1], 1 * n + 1)
                last.wait(pe, ("f", 0))
                wide = EXPERTS + ER
                for t in range(TILES):
                    done = nc.tensor.matmul(ps_f[:, 0, t * wide:(t + 1) * wide], xt[F1][:, t * P:(t + 1) * P], wgl[:],
                                            start=True, stop=True)
                done.then_inc(route_full, 1)
                last.used(("f", 0), routed, 7, dn, 7)

            def lora(s, dn, n):
                pe.wait_ge(routed, 7 * n + 7)
                last.wait(pe, ("f", 1))
                for t in range(TILES):
                    done = nc.tensor.transpose(ps_f[0:ER, 1, t * P:(t + 1) * P], low[:, t, :], ident[:])
                done.then_inc(lora_full, 1)
                last.used(("f", 1), lora_done, 1, dn, 1)

            def expert(s, dn, n, m):
                if m == 0:
                    pe.wait_ge(lora_done, 1 * n + 1)
                last.wait(pe, ("f", m % 2))
                nc.tensor.matmul(ps_f[:, m % 2, :], wi[:, m * P:(m + 1) * P], xt[F1][:], start=True, stop=False)
                nc.tensor.matmul(ps_f[:, m % 2, :], wlb[:, m * P:(m + 1) * P], lowt[:], start=False,
                                 stop=True).then_inc(exp_full, 1)
                last.used(("f", m % 2), relued, HB, dn, m + 1)

            def down(s, dn, n):
                if s == F0:
                    pe.wait_ge(gelued, 2 * n + 2)
                else:
                    pe.wait_ge(relued, HB * n + HB)
                last.wait(pe, ("f", 0))
                w = w3 if s == F0 else wout
                for t in range(TILES):
                    for k in range(HB):
                        done = nc.tensor.matmul(ps_f[:, 0, t * D:(t + 1) * D], hid[:, k, t * P:(t + 1) * P], w[:, k, :],
                                                start=k == 0, stop=k == HB - 1)
                done.then_inc(out_full[s], 1)
                last.used(("f", 0), ln[s], 5, dn, 1)

            walk(pe, dict(qkv=qkv, pass1=pass1, maxima=maxima, pass2=pass2, values=values, outputs=outputs,
                          merge=merge, project=project, turn=turn, gated=gated_, hidden=hidden, route=route,
                          lora=lora, expert=expert, down=down), last)


def kernel(**inputs):
    import concourse.bacc as bacc
    from concourse.bass_utils import run_bass_kernel_spmd

    a = {k: np.asarray(t) for k, t in inputs.items()}
    x = a["L0_attn_hidden_states"].reshape(BATCH * SEQ, D)

    def by_dim(w):
        return w.reshape(*w.shape[:-1], HEADS, HD).swapaxes(-1, -2).reshape(w.shape)

    def blocks(w):
        return w.reshape(-1, P, w.shape[-1]).transpose(1, 0, 2)

    def column(w):
        return w.reshape(-1, P).T

    wqkv, bqkv = a["L1_attn_W_qkv"], a["L1_attn_b_qkv"]
    lay = {
        "x": x,
        "xt": x.T,
        "qk_a": np.stack([a["L0_attn_q_a"], a["L0_attn_k_a"]]).transpose(3, 1, 0, 2),
        "qk_b": np.stack([a["L0_attn_q_b"], a["L0_attn_k_b"]]).transpose(2, 1, 0, 3),
        "v_w0": a["L0_attn_v_w"].T,
        "o_w0": a["L0_attn_o_w"].T,
        "w12": np.stack([a["L0_ffn_w1_w"].T, a["L0_ffn_w2_w"].T], axis=1),
        "wh": np.stack([blocks(a["L0_ffn_h1_w"].T), blocks(a["L0_ffn_h2_w"].T)], axis=1),
        "w3": blocks(a["L0_ffn_w3_w"].T),
        "qk_w1": np.stack([by_dim(wqkv[:, 0:D]), by_dim(wqkv[:, D:2 * D])], axis=1),
        "v_w1": wqkv[:, 2 * D:],
        "o_w1": a["L1_attn_W_out"],
        "wi": a["L1_ffn_wi_W"].T,
        "gl": np.concatenate([a["L1_ffn_gate_W"].T, a["L1_ffn_lora_A"].reshape(ER, D).T], axis=1),
        "lb": a["L1_ffn_lora_B"].transpose(0, 2, 1).reshape(ER, HID),
        "wo": blocks(a["L1_ffn_wo_W"].T),
        "cols": np.concatenate([column(t) for t in (
            a["L0_ffn_w1_s"], a["L0_ffn_w2_s"], a["L0_ffn_h1_s"], a["L0_ffn_h2_s"], a["L1_ffn_wi_b"],
            by_dim(bqkv[0:D]), by_dim(bqkv[D:2 * D]))], axis=1),
        "rows": np.concatenate([a["L0_attn_v_b"], a["L0_attn_o_b"], a["L0_ffn_w3_s"], bqkv[2 * D:],
                                a["L1_attn_b_out"], a["L1_ffn_gate_b"], a["L1_ffn_wo_b"]]),
    }
    nc = bacc.Bacc("TRN2", target_bir_lowering=False, num_devices=1)
    arrays, aps = {}, {}
    for name, t in lay.items():
        arrays[f"in_{name}"] = np.ascontiguousarray(t)
        aps[name] = nc.dram_tensor(f"in_{name}", t.shape, F32, kind="ExternalInput").ap()
    out = nc.dram_tensor("out", (BATCH * SEQ, D), F32, kind="ExternalOutput").ap()
    build(nc, aps, out)
    got = run_bass_kernel_spmd(nc, [arrays], core_ids=[0])
    return got.results[0]["out"].reshape(BATCH, SEQ, D)
```

```python
from contextlib import ExitStack

import numpy as np

import concourse.bass as bass
from concourse import mybir

F32 = mybir.dt.float32
BF16 = mybir.dt.bfloat16
ALU = mybir.AluOpType
ACT = mybir.ActivationFunctionType
AX = mybir.AxisListType.X

P = 128
D = 128
HEADS = 16
HD = D // HEADS
SEQ = 256
BATCH = 16
SEQS = 2
TOK = SEQS * SEQ
TILES = TOK // P
CHUNKS = BATCH // SEQS
QB = SEQ // P
GROUP = 4
GROUPS = HEADS // GROUP
PARTS = 3
ROWS = PARTS * PARTS * HD
ROWSM = ROWS + PARTS
HID = 512
HB = HID // P
RANK = 64
EXPERTS = 8
LORA = 4
ER = EXPERTS * LORA
EPS = 1e-5
MASKED = -3.0e38
TWO_ONES = float(np.array([0x3F803F80], np.uint32).view(np.float32)[0])
DMA = 16


COLS = ["w1_s", "w2_s", "h1_s", "h2_s", "wi_b", "q_b", "k_b"]
COL_AT = {n: sum(1 if m in ("q_b", "k_b") else HB for m in COLS[:i]) for i, n in enumerate(COLS)}
NCOLS = COL_AT["k_b"] + 1
ROWS_OF = {"v_b0": D, "o_b0": D, "w3_s": D, "v_b1": D, "o_b1": D, "gate_b": EXPERTS, "wo_b": D}
ROW_AT = {n: sum(list(ROWS_OF.values())[:i]) for i, n in enumerate(ROWS_OF)}
NROW = sum(ROWS_OF.values())

A0, F0, A1, F1 = range(4)
BANKS1 = {A0: 3, A1: 4}


def evenly(start, end, steps):
    return [(start + (end - start) * (i + 0.5) / len(steps), step) for i, step in enumerate(steps)]


def pass1(stage, dn, b):
    return [("pass1", stage, dn, b, j, u) for j in range(GROUPS) for u in range(BANKS1[stage])]


def pass2(stage, dn, b):
    steps = []
    for j in range(GROUPS):
        for g in range(GROUP):
            steps.append(("pass2", stage, dn, b, j, g))
            if j and g == 1:
                steps.append(("values", stage, dn, b, j - 1))
    return steps


def hidden(layer, dn):
    return [("hidden", F0, dn, layer, m, k) for m in range(HB) for k in range(HB)]


def order():
    at = []
    at += evenly(0.0, 1.0, pass2(A1, -1, 0)) + evenly(0.0, 0.72, pass1(A1, -1, 1)) + [(0.78, ("maxima", A1, -1, 1))]
    at += [(0.0, ("load", A0, 1)), (0.06, ("values", A0, 0, 1, GROUPS - 1)), (0.09, ("outputs", A0, 0, 1, 0)),
           (0.12, ("outputs", A0, 0, 1, 1)), (0.15, ("merge", A0, 0)), (0.19, ("project", A0, 0)), (0.22, ("sum", A0, 0)),
           (0.28, ("norm", A0, 0)), (0.32, ("turn", A0, 0)),
           (0.40, ("resid", A0, 1)), (0.40, ("qkv", A0, 1, 0)), (0.44, ("split", A0, 1, 0)), (0.50, ("qkv", A0, 1, 1)),
           (0.54, ("split", A0, 1, 1)), (0.60, ("qkv", A0, 1, 2)), (0.62, ("split", A0, 1, 2))]
    at += evenly(0.0, 0.12, [("expert", F1, -2, m) for m in range(HB)])
    at += evenly(0.13, 0.28, [("down", F1, -2, t) for t in range(TILES)])
    at += [(0.33, ("sum", F1, -2)), (0.36, ("norm", F1, -2)), (0.6, ("store", F1, -2))]
    at += evenly(0.36, 0.68, [("gated", F0, 0, m, side) for m in range(HB) for side in range(2)])
    at += evenly(0.70, 1.30, hidden(0, 0)) + [(1.33, ("gelu", F0, 0, 0))]
    at += evenly(1.0, 2.0, pass2(A1, -1, 1)) + evenly(1.0, 1.72, pass1(A0, 1, 0)) + [(1.78, ("maxima", A0, 1, 0))]
    at += [(1.06, ("values", A1, -1, 0, GROUPS - 1)), (1.12, ("outputs", A1, -1, 0, 0)), (1.2, ("outputs", A1, -1, 0, 1))]
    at += evenly(1.48, 2.1, hidden(1, 0)) + [(2.14, ("gelu", F0, 0, 1))]
    at += evenly(2.0, 3.0, pass2(A0, 1, 0)) + evenly(2.0, 2.66, pass1(A0, 1, 1)) + [(2.72, ("maxima", A0, 1, 1))]
    at += [(2.06, ("values", A1, -1, 1, GROUPS - 1)), (2.10, ("outputs", A1, -1, 1, 0)), (2.14, ("outputs", A1, -1, 1, 1)),
           (2.19, ("merge", A1, -1)), (2.24, ("project", A1, -1)), (2.28, ("sum", A1, -1)), (2.36, ("norm", A1, -1)),
           (2.42, ("turn", A1, -1))]
    at += evenly(2.28, 2.5, [("down", F0, 0, t) for t in range(TILES)])
    at += [(2.52, ("sum", F0, 0)), (2.62, ("norm", F0, 0)), (2.66, ("turn", F0, 0)), (2.70, ("resid", A1, 0)),
           (2.76, ("qkv", A1, 0, 0)), (2.80, ("split", A1, 0, 0)), (2.86, ("qkv", A1, 0, 1)),
           (2.90, ("split", A1, 0, 1)), (2.96, ("qkv", A1, 0, 2)), (2.98, ("split", A1, 0, 2))]
    at += evenly(3.0, 4.0, pass2(A0, 1, 1)) + evenly(3.3, 3.76, pass1(A1, 0, 0)) + [(3.82, ("maxima", A1, 0, 0))]
    at += [(3.06, ("values", A0, 1, 0, GROUPS - 1)), (3.12, ("outputs", A0, 1, 0, 0)), (3.2, ("outputs", A0, 1, 0, 1)),
           (3.1, ("resid", F1, -1)), (3.1, ("route", F1, -1)), (3.4, ("lora", F1, -1))]
    return [step for _, step in sorted(at, key=lambda t: t[0])]


ORDER = order()
BEHIND = max(-step[2] for step in ORDER)
AHEAD = max(step[2] for step in ORDER)


class Last:

    def __init__(self):
        self.c, self.of = 0, {}

    def next_chunk(self, c):
        self.c = c
        self.of = {key: (s, per, dn - 1, k) for key, (s, per, dn, k) in self.of.items()}

    def used(self, key, sem, per, dn, k):
        self.of[key] = (sem, per, dn, k)

    def wait(self, engine, key):
        if key in self.of:
            sem, per, dn, k = self.of[key]
            engine.wait_ge(sem, per * (self.c + dn) + k)


def walk(engine, steps, last=None):

    def round_(c, present):
        if last:
            last.next_chunk(c)
        for name, stage, dn, *args in ORDER:
            if name in steps and present(dn):
                steps[name](stage, dn, c + dn, *args)

    def some(c):
        round_(c, lambda dn: 0 <= c + dn < CHUNKS)

    for c in range(-AHEAD, BEHIND + 1):
        some(c)
    before = dict(last.of) if last else None
    with engine.Fori(BEHIND + 1, CHUNKS - AHEAD) as c:
        round_(c, lambda dn: True)
        assert not last or before == last.of, (before, last.of)
    for c in range(CHUNKS - AHEAD, CHUNKS + BEHIND):
        some(c)


def build(nc, d_in, out):
    ctx = ExitStack()
    with ctx:
        def sb(name, shape, dt=F32):
            return ctx.enter_context(nc.sbuf_tensor(name, shape, dt))

        def ps(name, shape):
            return ctx.enter_context(nc.psum_tensor(name, shape, F32))

        def sem(name):
            return ctx.enter_context(nc.semaphore(name))

        ps_s1 = ps("ps_s1", [P, 2, 512])
        ps_s2 = ps("ps_s2", [P, 2, 512])
        ps_o = ps("ps_o", [P, 512])
        ps_m = ps("ps_m", [P, 512])
        ps_f = ps("ps_f", [P, 2, 512])

        wqb = sb("wqb", [RANK, HEADS, 2, HD])
        wq = {s: sb(f"wq{s}", [P, 2, D]) for s in (A0, A1)}
        wv = {s: sb(f"wv{s}", [P, D]) for s in (A0, A1)}
        wo = {s: sb(f"wo{s}", [P, D]) for s in (A0, A1)}
        w12 = sb("w12", [P, 2, HID])
        wh = sb("wh", [P, 2, HB, HID])
        w3 = sb("w3", [P, HB, D])
        wi = sb("wi", [P, HID])
        wgl = sb("wgl", [P, EXPERTS + ER])
        wlb = sb("wlb", [ER, HID])
        wout = sb("wout", [P, HB, D])
        cols = sb("cols", [P, NCOLS])
        rows = sb("rows", [P, NROW])
        half_s = sb("half_s", [P, HB])
        gate_s = sb("gate_s", [P, HB])
        ident = sb("ident", [P, P])
        identb = sb("identb", [P, P], BF16)
        above = sb("above", [P, P], BF16)
        ranks = sb("ranks", [P, EXPERTS])
        minus_half = sb("minus_half", [P, TILES])
        dve_carrier = sb("dve_carrier", [P, 4])
        pool_carrier = sb("pool_carrier", [P, SEQS * GROUPS])

        def col(name, i=0):
            return cols[:, COL_AT[name] + i:COL_AT[name] + i + 1]

        def row(name):
            return rows[:, ROW_AT[name]:ROW_AT[name] + ROWS_OF[name]]

        x = {s: sb(f"x{s}", [P, TILES, D]) for s in (A0, F0, A1, F1)}
        x["out"] = sb("xout", [P, TILES, D])
        xt = {s: sb(f"xt{s}", [P, TOK]) for s in (A0, F0, A1, F1)}
        resid = {s: sb(f"resid{s}", [P, TILES, D]) for s in (A0, A1, F1)}
        resid[F0] = x[F0]
        into = {A0: F0, F0: A1, A1: F1, F1: "out"}
        ln_sum = sb("ln_sum", [P, TILES, D])
        ln_parts = sb("ln_parts", [P, TILES, 6])
        ln_stat = {s: sb(f"ln_stat{s}", [P, TILES, 2]) for s in range(4)}
        ln_var = {s: sb(f"ln_var{s}", [P, TILES]) for s in range(4)}
        ln_rstd = {s: sb(f"ln_rstd{s}", [P, TILES]) for s in range(4)}

        split = sb("split", [P, 2, PARTS, TOK], BF16)
        rest = sb("rest", [P, 2, TOK])
        qrow = {s: sb(f"qrow{s}", [P, HEADS, TOK], BF16) for s in (A0, A1)}
        krow = {s: sb(f"krow{s}", [P, HEADS, TOK], BF16) for s in (A0, A1)}
        v = {s: sb(f"v{s}", [P, TILES, HEADS, 32]) for s in (A0, A1)}
        top = {s: sb(f"top{s}", [P, SEQS, QB, HEADS]) for s in (A0, A1)}
        tsplit = sb("tsplit", [HEADS, SEQS, PARTS, SEQ], BF16)
        trest = sb("trest", [HEADS, SEQ])
        prob = sb("prob", [P, 2, GROUP, QB * SEQ])
        osum = sb("osum", [P, SEQS, GROUPS, SEQ])
        recip = sb("recip", [P, HEADS])
        y = sb("y", [P, TILES, D])
        yt = sb("yt", [P, TOK])

        hid = sb("hid", [P, HB, TOK])
        gel = sb("gel", [P, HB, TOK])
        hidden_of = (gel, hid)
        wqa = prob[0:RANK].rearrange("p a g t -> p (a g t)").rearrange("p (h s d) -> p h s d", h=HEADS, s=2)
        w3raw = gel[:, 0, :].rearrange("p (k d) -> p k d", k=HB)
        logit = sb("logit", [P, TILES, EXPERTS])
        best = sb("best", [P, TILES])
        pick = sb("pick", [P, TILES, EXPERTS])
        first = sb("first", [P, TILES])
        low = sb("low", [P, TILES, ER])
        lowt = sb("lowt", [ER, TOK])

        weights = sem("weights")
        weights0 = sem("weights0")
        made = sem("made")
        folded = sem("folded")
        wready = sem("wready")
        loaded = sem("loaded")
        stored = sem("stored")

        def per_stage(name, stages=(A0, A1)):
            return {s: sem(f"{name}{s}") for s in stages}

        proj_full = per_stage("proj_full")
        part1 = per_stage("part1")
        parts = per_stage("parts")
        v_done = per_stage("v_done")
        spread = per_stage("spread")
        s1_full = per_stage("s1_full")
        maxed = per_stage("maxed")
        top_full = per_stage("top_full")
        tparts = per_stage("tparts")
        trows = per_stage("trows")
        s2_full = per_stage("s2_full")
        exped = per_stage("exped")
        causal = sem("causal")
        pv_full = per_stage("pv_full")
        o_done = per_stage("o_done")
        ot_full = per_stage("ot_full")
        scaled = per_stage("scaled")
        yt_full = per_stage("yt_full")
        yt_done = per_stage("yt_done")
        out_full = per_stage("out_full", range(4))
        ln = per_stage("ln", range(4))
        rstd = per_stage("rstd", range(4))
        biased = per_stage("biased", (A0, A1, F1))
        xt_full = per_stage("xt_full", range(3))
        xt_done = per_stage("xt_done", range(3))
        gate_full = sem("gate_full")
        tanhed = sem("tanhed")
        gated = sem("gated")
        hid_full = sem("hid_full")
        hid_done = sem("hid_done")
        gelued = sem("gelued")
        route_full = sem("route_full")
        routed = sem("routed")
        lora_full = sem("lora_full")
        lora_done = sem("lora_done")
        exp_full = sem("exp_full")
        relued = sem("relued")

        S1 = {s: SEQS * GROUPS * BANKS1[s] for s in BANKS1}
        NSPREAD = 2 * PARTS * PARTS * DMA
        S2 = SEQS * HEADS
        NWEIGHTS = 14 * DMA

        block = ctx.enter_context(nc.Block())

        @block.sync
        def _(sp):
            sp.dma_start(wqa, d_in["qk_a"]).then_inc(weights0, DMA)
            sp.dma_start(wqb[:], d_in["qk_b"]).then_inc(weights0, DMA)

            def load(s, dn, n):
                if not isinstance(n, int) or n:
                    sp.wait_ge(proj_full[A0], 3 * n)
                    sp.wait_ge(biased[A0], 1 * n)
                sp.dma_start(xt[A0][:], d_in["xt"][:, bass.ts(n, TOK)]).then_inc(loaded, DMA)
                sp.dma_start(x[A0][:], d_in["x"][bass.ts(n, TOK), :].rearrange("(t p) d -> p t d", p=P)).then_inc(loaded, DMA)

            def spread_rows(s, dn, n, side):
                if side < 2:
                    dst = (qrow, krow)[side][s]
                    sp.wait_ge(parts[s], 6 * n + 3 * side + 3)
                    for i in range(PARTS):
                        for j in range(PARTS):
                            r = (i * PARTS + j) * HD
                            src = split[:, side, (i, j)[side], :]
                            sp.dma_start(dst[r:r + HD, :, :], src).then_inc(spread[s], DMA)

            def maxima(s, dn, n, b):
                sp.wait_ge(tparts[s], 8 * n + 4 * b + 4)
                for i in range(PARTS):
                    sp.dma_start(qrow[s][ROWS + i:ROWS + i + 1, :, b * SEQ:(b + 1) * SEQ],
                                 tsplit[:, b, i, :]).then_inc(trows[s], DMA)

            def store(s, dn, n):
                sp.wait_ge(ln[F1], 5 * n + 5)
                sp.dma_start(out[bass.ts(n, TOK), :].rearrange("(t p) d -> p t d", p=P), x["out"][:]).then_inc(stored, DMA)

            walk(sp, dict(load=load, split=spread_rows, maxima=maxima, store=store))
            sp.wait_ge(stored, CHUNKS * DMA)

        @block.gpsimd
        def _(pool):
            nc.gpsimd.memset(ident[:], 0.0)
            nc.gpsimd.memset(above[:], 0.0)
            nc.gpsimd.memset(minus_half[:], -0.5)
            nc.gpsimd.iota(ranks[:], pattern=[[1, EXPERTS]], base=-EXPERTS, channel_multiplier=0,
                           allow_small_or_imprecise_dtypes=True)
            for s in (A0, A1):
                nc.gpsimd.memset(v[s][:].rearrange("p t h c -> p (t h c)"), 1.0 if s == A0 else float(np.sqrt(D)))
            nc.gpsimd.memset(identb[:], 0.0).then_inc(made, 1)
            pool.wait_ge(made, 1)
            nc.gpsimd.affine_select(out=ident[:], in_=ident[:], compare_op=ALU.not_equal, fill=1.0,
                                    base=0, pattern=[[-1, P]], channel_multiplier=1)
            nc.gpsimd.affine_select(out=identb[:], in_=identb[:], compare_op=ALU.not_equal, fill=1.0,
                                    base=0, pattern=[[-1, P]], channel_multiplier=1)
            nc.gpsimd.affine_select(out=above[:], in_=above[:], compare_op=ALU.is_ge, fill=MASKED,
                                    base=0, pattern=[[-1, P]], channel_multiplier=1).then_inc(made, 1)
            pool.wait_ge(weights, NWEIGHTS)

            def add_bias(s, dn, n):
                if s == A0:
                    pool.wait_ge(loaded, 2 * DMA * n + 2 * DMA)
                elif s == A1:
                    pool.wait_ge(ln[F0], 5 * n + 5)
                else:
                    pool.wait_ge(ln[A1], 5 * n + 5)
                if not isinstance(n, int) or n:
                    pool.wait_ge(ln[s], 5 * n - 4)
                bias = row({A0: "o_b0", A1: "o_b1", F1: "wo_b"}[s])
                nc.gpsimd.tensor_tensor(resid[s][:], x[s][:], bias.unsqueeze(1).to_broadcast([P, TILES, D]),
                                        ALU.add).then_inc(biased[s], 1)

            def deviation(s, dn, n):
                pool.wait_ge(ln[s], 5 * n + 4)
                nc.gpsimd.tensor_tensor(ln_rstd[s][:], ln_var[s][:], minus_half[:], ALU.pow).then_inc(rstd[s], 1)

            def mask(s, dn, n, b, j, g):
                if s == A0 and g == GROUP - 1:
                    pool.wait_ge(exped[A0], S2 * n + HEADS * b + GROUP * (j + 1))
                    k = GROUPS * b + j
                    nc.gpsimd.tensor_tensor(pool_carrier[:, k:k + 1], minus_half[:, 0:1], minus_half[:, 0:1], ALU.add)
                    diag = prob[:, j % 2].rearrange("p h (k q) -> p h k q", k=2)[:, :, :, 0:P]
                    nc.gpsimd.affine_select(out=diag, in_=diag, compare_op=ALU.is_ge, fill=0.0, base=0,
                                            pattern=[[0, GROUP], [0, QB], [1, P]],
                                            channel_multiplier=-1).then_inc(causal, 1)

            walk(pool, dict(resid=add_bias, sum=deviation, pass2=mask))

        @block.scalar
        def _(act):
            for dst, name in ((wv[A0][:], "v_w0"), (wo[A0][:], "o_w0"), (cols[:], "cols"), (w12[:], "w12"),
                              (wh[:], "wh"), (w3raw, "w3"), (wq[A1][:], "qk_w1"), (wv[A1][:], "v_w1"),
                              (wo[A1][:], "o_w1"), (wi[:], "wi"), (wgl[:], "gl"), (wlb[:], "lb"), (wout[:], "wo")):
                act.dma_start(dst, d_in[name]).then_inc(weights, DMA)
            act.dma_start(rows[:], d_in["rows"].partition_broadcast(P)).then_inc(weights, DMA)
            act.wait_ge(wready, 5)
            last = Last()

            def qkv(s, dn, n, side):
                if side < 2:
                    act.wait_ge(proj_full[s], 3 * n + side + 1)
                    nc.scalar.activation(split[:, side, 0, :], ps_m[:], ACT.Identity,
                                         bias=0.0 if s == A0 else col(("q_b", "k_b")[side])).then_inc(part1[s], 1)

            def pass2(s, dn, n, b, j, g):
                wide = SEQ + P if s == A0 else QB * SEQ
                if g == 0:
                    last.wait(act, ("prob", j % 2))
                    last.used(("prob", j % 2), pv_full[s], SEQS * GROUPS, dn, GROUPS * b + j + 1)
                act.wait_ge(s2_full[s], S2 * n + HEADS * b + GROUP * j + g + 1)
                nc.scalar.activation(prob[:, j % 2, g, 0:wide], ps_s2[:, g % 2, 0:wide], ACT.Exp,
                                     scale=1.0 / float(np.sqrt(np.float32(HD))) if s == A0 else 1.0).then_inc(exped[s], 1)

            def values(s, dn, n, b, j):
                act.wait_ge(pv_full[s], SEQS * GROUPS * n + GROUPS * b + j + 1)
                nc.scalar.activation(osum[:, b, j, :], ps_o[:, 0:SEQ], ACT.Copy).then_inc(o_done[s], 1)

            def merge(s, dn, n):
                act.wait_ge(yt_full[s], 1 * n + 1)
                nc.scalar.activation(yt[:], ps_m[:], ACT.Copy).then_inc(yt_done[s], 1)

            def turn(s, dn, n):
                act.wait_ge(xt_full[s], 1 * n + 1)
                src = ps_f[:, 1, :] if s == F0 else ps_m[:]
                nc.scalar.activation(xt[into[s]][:], src, ACT.Copy).then_inc(xt_done[s], 1)

            def tanh(s, dn, n, m, side):
                if side == 0:
                    act.wait_ge(gate_full, 2 * HB * n + 2 * m + 1)
                    nc.scalar.activation(hid[:, m, :], ps_f[:, 0, :], ACT.Tanh, scale=half_s[:, m:m + 1]).then_inc(tanhed, 1)

            def gelu(s, dn, n, layer):
                act.wait_ge(hid_done, 2 * HB * n + HB * (layer + 1))
                nc.scalar.activation(hidden_of[layer][:], hidden_of[layer][:], ACT.Gelu).then_inc(gelued, 1)

            def lora(s, dn, n):
                act.wait_ge(lora_full, 1 * n + 1)
                nc.scalar.activation(lowt[:], ps_f[0:ER, 1, :], ACT.Copy).then_inc(lora_done, 1)

            def expert(s, dn, n, m):
                act.wait_ge(exp_full, HB * n + m + 1)
                nc.scalar.activation(hid[:, m, :], ps_f[:, m % 2, :], ACT.Relu, bias=col("wi_b", m)).then_inc(relued, 1)

            walk(act, dict(qkv=qkv, pass2=pass2, values=values, merge=merge, turn=turn, gated=tanh, gelu=gelu,
                           lora=lora, expert=expert), last)

        @block.vector
        def _(dve):
            for s in (A0, A1):
                nc.vector.memset(krow[s][64:96, :, :].rearrange("p h t -> p (h t)").bitcast(F32), TWO_ONES)
            dve.wait_ge(folded, 1)
            nc.vector.tensor_copy(wq[A0][:].rearrange("p a c -> p (a c)"), ps_m[:, 0:2 * D]).then_inc(wready, 1)
            dve.wait_ge(weights, NWEIGHTS)
            nc.vector.tensor_scalar(half_s[:], cols[:, COL_AT["w1_s"]:COL_AT["w1_s"] + HB], 0.5, None, ALU.mult).then_inc(wready, 1)
            dve.wait_ge(wready, 2)
            nc.vector.tensor_tensor(gate_s[:], half_s[:], cols[:, COL_AT["w2_s"]:COL_AT["w2_s"] + HB], ALU.mult).then_inc(wready, 1)
            nc.vector.tensor_tensor(w3[:], w3raw, row("w3_s").unsqueeze(1).to_broadcast([P, HB, D]), ALU.mult).then_inc(wready, 1)
            dve.wait_ge(made, 2)
            nc.vector.memset(recip[:], 0.0).then_inc(wready, 1)
            last = Last()

            def split_(s, dn, n, side):
                if side < 2:
                    r = rest[:, side, :]
                    dve.wait_ge(part1[s], 2 * n + side + 1)
                    nc.vector.scalar_tensor_tensor(out=r, in0=ps_m[:], scalar=0.0 if s == A0 else col(("q_b", "k_b")[side]),
                                                   in1=split[:, side, 0, :], op0=ALU.add,
                                                   op1=ALU.subtract).then_inc(parts[s], 1)
                    dve.wait_ge(parts[s], 6 * n + 3 * side + 1)
                    nc.vector.tensor_copy(split[:, side, 1, :], r).then_inc(parts[s], 1)
                    dve.wait_ge(parts[s], 6 * n + 3 * side + 2)
                    nc.vector.tensor_tensor(split[:, side, 2, :], r, split[:, side, 1, :],
                                            ALU.subtract).then_inc(parts[s], 1)
                    return
                dve.wait_ge(proj_full[s], 3 * n + 3)
                bias = row("v_b0" if s == A0 else "v_b1").rearrange("p (h c) -> p h c", c=HD)
                for t in range(TILES):
                    done = nc.vector.tensor_tensor(v[s][:, t, :, 0:HD], ps_m[:, t * D:(t + 1) * D].rearrange("p (h c) -> p h c", c=HD),
                                                   bias, ALU.add)
                done.then_inc(v_done[s], 1)

            def pass1(s, dn, n, b, j, u):
                k = (GROUPS * b + j) * BANKS1[s] + u
                dve.wait_ge(s1_full[s], S1[s] * n + k + 1)
                bank = ps_s1[:, k % 2, :]
                h = GROUP * j
                if s == A0 and u == 0:
                    dst, src = top[s][:, b, 0, h:h + 4], bank.rearrange("p (h k) -> p h k", h=4)
                else:
                    qb, pair = (1, u - 1) if s == A0 else (u % 2, u // 2)
                    dst = top[s][:, b, qb, h + 2 * pair:h + 2 * pair + 2]
                    src = bank.rearrange("p (h k) -> p h k", h=2)
                nc.vector.tensor_reduce(out=dst, in_=src, axis=AX, op=ALU.max, negate=True).then_inc(maxed[s], 1)

            def maxima(s, dn, n, b):
                src = ps_m[0:HEADS, 0:SEQ]
                t = tsplit[:, b]
                dve.wait_ge(top_full[s], 2 * n + b + 1)
                nc.vector.tensor_copy(t[:, 0, :], src).then_inc(tparts[s], 1)
                dve.wait_ge(tparts[s], 8 * n + 4 * b + 1)
                nc.vector.tensor_tensor(trest[:], src, t[:, 0, :], ALU.subtract).then_inc(tparts[s], 1)
                dve.wait_ge(tparts[s], 8 * n + 4 * b + 2)
                nc.vector.tensor_copy(t[:, 1, :], trest[:]).then_inc(tparts[s], 1)
                dve.wait_ge(tparts[s], 8 * n + 4 * b + 3)
                nc.vector.tensor_tensor(t[:, 2, :], trest[:], t[:, 1, :], ALU.subtract).then_inc(tparts[s], 1)

            def outputs(s, dn, n, b, qb):
                i = QB * b + qb
                src = ps_m[:].rearrange("p (h c) -> p h c", c=32)
                dve.wait_ge(ot_full[s], 4 * n + i + 1)
                nc.vector.reciprocal(recip[:], src[:, :, HD]).then_inc(scaled[s], 1)
                dve.wait_ge(scaled[s], 8 * n + 2 * i + 1)
                nc.vector.tensor_tensor(y[:, i, :].rearrange("p (h c) -> p h c", c=HD), src[:, :, 0:HD],
                                        recip[:].unsqueeze(2).to_broadcast([P, HEADS, HD]),
                                        ALU.mult).then_inc(scaled[s], 1)

            def sum_(s, dn, n):
                src = ps_m[:] if s in (A0, A1) else ps_f[:, 0, :]
                dve.wait_ge(out_full[s], 1 * n + 1)
                last.wait(dve, "ln_sum")
                last.used("ln_sum", ln[s], 5, dn, 5)
                if s == F0:
                    dve.wait_ge(ln[A0], 5 * n + 5)
                else:
                    dve.wait_ge(biased[s], 1 * n + 1)
                nc.vector.tensor_tensor(ln_sum[:], src.rearrange("p (t d) -> p t d", t=TILES), resid[s][:],
                                        ALU.add).then_inc(ln[s], 1)
                dve.wait_ge(ln[s], 5 * n + 1)
                for t in range(TILES):
                    done = nc.vector.bn_stats(ln_parts[:, t, :], ln_sum[:, t, :])
                done.then_inc(ln[s], 1)
                dve.wait_ge(ln[s], 5 * n + 2)
                nc.vector.memset(dve_carrier[:, s:s + 1], 0.0)
                for t in range(TILES):
                    done = nc.vector.bn_aggr(ln_stat[s][:, t, :], ln_parts[:, t, :])
                done.then_inc(ln[s], 1)
                dve.wait_ge(ln[s], 5 * n + 3)
                nc.vector.tensor_scalar(ln_var[s][:], ln_stat[s][:, :, 1], EPS, None, ALU.add).then_inc(ln[s], 1)

            def norm(s, dn, n):
                dve.wait_ge(rstd[s], 1 * n + 1)
                if s == F1 and (not isinstance(n, int) or n):
                    dve.wait_ge(stored, DMA * n)
                for t in range(TILES):
                    done = nc.vector.tensor_scalar(x[into[s]][:, t, :], ln_sum[:, t, :], ln_stat[s][:, t, 0:1],
                                                   ln_rstd[s][:, t:t + 1], ALU.subtract, ALU.mult)
                done.then_inc(ln[s], 1)

            def gate(s, dn, n, m, side):
                if side == 0:
                    dve.wait_ge(tanhed, HB * n + m + 1)
                    nc.vector.scalar_tensor_tensor(out=hid[:, m, :], in0=hid[:, m, :], scalar=1.0, in1=ps_f[:, 0, :],
                                                   op0=ALU.add, op1=ALU.mult).then_inc(gated, 1)
                    return
                dve.wait_ge(gate_full, 2 * HB * n + 2 * m + 2)
                dve.wait_ge(gated, 2 * HB * n + 2 * m + 1)
                nc.vector.scalar_tensor_tensor(out=hid[:, m, :], in0=ps_f[:, 1, :], scalar=gate_s[:, m:m + 1],
                                               in1=hid[:, m, :], op0=ALU.mult, op1=ALU.mult).then_inc(gated, 1)

            def hidden(s, dn, n, layer, m, k):
                if k < HB - 1:
                    return
                dve.wait_ge(hid_full, 2 * HB * n + HB * layer + m + 1)
                nc.vector.tensor_scalar(hidden_of[layer][:, m, :], ps_f[:, m % 2, :], col(("h1_s", "h2_s")[layer], m), None,
                                        ALU.mult).then_inc(hid_done, 1)

            def route(s, dn, n):
                src = ps_f[:, 0, 0:TILES * (EXPERTS + ER)].rearrange("p (t c) -> p t c", t=TILES)
                wide = [P, TILES, EXPERTS]

                def step(k, ins):
                    ins.then_inc(routed, 1)
                    dve.wait_ge(routed, 7 * n + k)

                dve.wait_ge(route_full, 1 * n + 1)
                step(1, nc.vector.tensor_tensor(logit[:], src[:, :, 0:EXPERTS], row("gate_b").unsqueeze(1).to_broadcast(wide), ALU.add))
                step(2, nc.vector.tensor_reduce(out=best[:], in_=logit[:], axis=AX, op=ALU.max))
                step(3, nc.vector.tensor_tensor(pick[:], logit[:], best[:].unsqueeze(2).to_broadcast(wide), ALU.is_ge))
                step(4, nc.vector.tensor_tensor(pick[:], pick[:], ranks[:].unsqueeze(1).to_broadcast(wide), ALU.mult))
                step(5, nc.vector.tensor_reduce(out=first[:], in_=pick[:], axis=AX, op=ALU.min))
                step(6, nc.vector.tensor_tensor(pick[:], pick[:], first[:].unsqueeze(2).to_broadcast(wide), ALU.is_equal))
                nc.vector.tensor_tensor(low[:].rearrange("p t (e r) -> p t e r", r=LORA),
                                        src[:, :, EXPERTS:].rearrange("p t (e r) -> p t e r", r=LORA),
                                        pick[:].unsqueeze(3).to_broadcast([P, TILES, EXPERTS, LORA]),
                                        ALU.mult).then_inc(routed, 1)

            walk(dve, dict(split=split_, pass1=pass1, maxima=maxima, outputs=outputs, sum=sum_, norm=norm, gated=gate,
                           hidden=hidden, route=route), last)

        @block.tensor
        def _(pe):
            pe.wait_ge(weights0, 2 * DMA)
            for side in range(2):
                for h in range(HEADS):
                    at = ps_m[:, side * D:(side + 1) * D].rearrange("p (c h) -> p c h", h=HEADS)[:, :, h]
                    done = nc.tensor.matmul(at, wqa[:, h, side, :], wqb[:, h, side, :], start=True, stop=True)
            done.then_inc(folded, 1)
            pe.wait_ge(wready, 5)
            last = Last()

            def qkv(s, dn, n, side):
                if side == 0:
                    if s == A0:
                        pe.wait_ge(loaded, 2 * DMA * n + 2 * DMA)
                    else:
                        pe.wait_ge(xt_done[F0], 1 * n + 1)
                last.wait(pe, "m")
                if side < 2:
                    nc.tensor.matmul(ps_m[:], wq[s][:, side, :], xt[s][:], start=True, stop=True).then_inc(proj_full[s], 1)
                    last.used("m", parts[s], 6, dn, 3 * side + 1)
                    return
                for t in range(TILES):
                    done = nc.tensor.matmul(ps_m[:, t * D:(t + 1) * D], xt[s][:, t * P:(t + 1) * P], wv[s][:],
                                            start=True, stop=True)
                done.then_inc(proj_full[s], 1)
                last.used("m", v_done[s], 1, dn, 1)

            def pass1(s, dn, n, b, j, u):
                if b == 0 and j == 0 and u == 0:
                    pe.wait_ge(spread[s], NSPREAD * n + NSPREAD)

                def keys(h, blocks):
                    return krow[s][0:ROWS, h, b * SEQ:b * SEQ + blocks * P]

                def queries(h, qb):
                    return qrow[s][0:ROWS, h, b * SEQ + qb * P:b * SEQ + (qb + 1) * P]

                def mask(at):
                    return nc.tensor.matmul(at, identb[:], above[:], start=False, stop=True, skip_group_check=True)

                k = (GROUPS * b + j) * BANKS1[s] + u
                bank = ps_s1[:, k % 2, :]
                last.wait(pe, ("s1", k % 2))
                if s == A0 and u == 0:
                    for g in range(GROUP):
                        at = bank[:, g * P:(g + 1) * P]
                        nc.tensor.matmul(at, queries(GROUP * j + g, 0), keys(GROUP * j + g, 1), start=True, stop=False,
                                         skip_group_check=True)
                        done = mask(at)
                else:
                    qb, pair = (1, u - 1) if s == A0 else (u % 2, u // 2)
                    for g in range(2):
                        h = GROUP * j + 2 * pair + g
                        at = bank[:, g * SEQ:(g + 1) * SEQ]
                        done = nc.tensor.matmul(at, queries(h, qb), keys(h, 2), start=True, stop=s == A1,
                                                skip_group_check=True)
                        if s == A0:
                            done = mask(at[:, P:])
                done.then_inc(s1_full[s], 1)
                last.used(("s1", k % 2), maxed[s], S1[s], dn, k + 1)

            def maxima(s, dn, n, b):
                pe.wait_ge(maxed[s], S1[s] * n + S1[s] // SEQS * (b + 1))
                last.wait(pe, "m")
                for qb in range(QB):
                    done = nc.tensor.transpose(ps_m[0:HEADS, qb * P:(qb + 1) * P], top[s][:, b, qb, :], ident[:])
                done.then_inc(top_full[s], 1)
                last.used("m", tparts[s], 8, dn, 4 * b + 2)

            def pass2(s, dn, n, b, j, g):
                if j == 0 and g == 0:
                    pe.wait_ge(trows[s], 2 * PARTS * DMA * n + PARTS * DMA * (b + 1))
                h = GROUP * j + g
                bank = ps_s2[:, g % 2, :]
                last.wait(pe, ("s2", g % 2))
                for kb in range(QB):
                    q0 = P * kb if s == A0 else 0
                    done = nc.tensor.matmul(bank[:, kb * SEQ:(kb + 1) * SEQ - q0],
                                            krow[s][0:ROWSM, h, b * SEQ + kb * P:b * SEQ + (kb + 1) * P],
                                            qrow[s][0:ROWSM, h, b * SEQ + q0:(b + 1) * SEQ], start=True, stop=True)
                done.then_inc(s2_full[s], 1)
                last.used(("s2", g % 2), exped[s], S2, dn, HEADS * b + h + 1)

            def values(s, dn, n, b, j):
                if s == A0:
                    pe.wait_ge(causal, SEQS * GROUPS * n + GROUPS * b + j + 1)
                else:
                    pe.wait_ge(exped[s], S2 * n + HEADS * b + GROUP * (j + 1))
                if b == 0 and j == 0:
                    pe.wait_ge(v_done[s], 1 * n + 1)
                last.wait(pe, "o")
                for kb in range(QB):
                    q0 = P * kb if s == A0 else 0
                    for g in range(GROUP):
                        done = nc.tensor.matmul(ps_o[32 * g:32 * g + 32, q0:SEQ], v[s][:, QB * b + kb, GROUP * j + g, :],
                                                prob[:, j % 2, g, kb * SEQ:(kb + 1) * SEQ - q0],
                                                start=kb == 0, stop=kb == QB - 1, skip_group_check=True)
                done.then_inc(pv_full[s], 1)
                last.used("o", o_done[s], SEQS * GROUPS, dn, GROUPS * b + j + 1)

            def outputs(s, dn, n, b, qb):
                if qb == 0:
                    pe.wait_ge(o_done[s], SEQS * GROUPS * n + GROUPS * (b + 1))
                last.wait(pe, "m")
                for j in range(GROUPS):
                    done = nc.tensor.transpose(ps_m[:, j * P:(j + 1) * P], osum[:, b, j, qb * P:(qb + 1) * P], ident[:])
                done.then_inc(ot_full[s], 1)
                last.used("m", scaled[s], 8, dn, 2 * (QB * b + qb) + 2)

            def merge(s, dn, n):
                pe.wait_ge(scaled[s], 8 * n + 8)
                last.wait(pe, "m")
                for t in range(TILES):
                    done = nc.tensor.transpose(ps_m[:, t * P:(t + 1) * P], y[:, t, :], ident[:])
                done.then_inc(yt_full[s], 1)
                last.used("m", yt_done[s], 1, dn, 1)

            def project(s, dn, n):
                pe.wait_ge(yt_done[s], 1 * n + 1)
                last.wait(pe, "m")
                for t in range(TILES):
                    done = nc.tensor.matmul(ps_m[:, t * D:(t + 1) * D], yt[:, t * P:(t + 1) * P], wo[s][:],
                                            start=True, stop=True)
                done.then_inc(out_full[s], 1)
                last.used("m", ln[s], 5, dn, 1)

            def turn(s, dn, n):
                key, bank = (("f", 1), ps_f[:, 1, :]) if s == F0 else ("m", ps_m[:])
                pe.wait_ge(ln[s], 5 * n + 5)
                last.wait(pe, key)
                for t in range(TILES):
                    done = nc.tensor.transpose(bank[:, t * P:(t + 1) * P], x[into[s]][:, t, :], ident[:])
                done.then_inc(xt_full[s], 1)
                last.used(key, xt_done[s], 1, dn, 1)

            def gate(s, dn, n, m, side):
                if m == 0 and side == 0:
                    pe.wait_ge(xt_done[A0], 1 * n + 1)
                last.wait(pe, ("f", side))
                nc.tensor.matmul(ps_f[:, side, :], w12[:, side, m * P:(m + 1) * P], xt[F0][:], start=True,
                                 stop=True).then_inc(gate_full, 1)
                last.used(("f", side), gated, 2 * HB, dn, 2 * m + 1 + side)

            def hidden(s, dn, n, layer, m, k):
                if k == 0:
                    if m == 0 and layer == 0:
                        pe.wait_ge(gated, 2 * HB * n + 2 * HB)
                    elif m == 0:
                        pe.wait_ge(gelued, 2 * n + 1)
                    last.wait(pe, ("f", m % 2))
                done = nc.tensor.matmul(ps_f[:, m % 2, :], wh[:, layer, k, m * P:(m + 1) * P], (hid, gel)[layer][:, k, :],
                                        start=k == 0, stop=k == HB - 1)
                if k == HB - 1:
                    done.then_inc(hid_full, 1)
                    last.used(("f", m % 2), hid_done, 2 * HB, dn, HB * layer + m + 1)

            def route(s, dn, n):
                pe.wait_ge(xt_done[A1], 1 * n + 1)
                last.wait(pe, ("f", 0))
                wide = EXPERTS + ER
                for t in range(TILES):
                    done = nc.tensor.matmul(ps_f[:, 0, t * wide:(t + 1) * wide], xt[F1][:, t * P:(t + 1) * P], wgl[:],
                                            start=True, stop=True)
                done.then_inc(route_full, 1)
                last.used(("f", 0), routed, 7, dn, 7)

            def lora(s, dn, n):
                pe.wait_ge(routed, 7 * n + 7)
                last.wait(pe, ("f", 1))
                for t in range(TILES):
                    done = nc.tensor.transpose(ps_f[0:ER, 1, t * P:(t + 1) * P], low[:, t, :], ident[:])
                done.then_inc(lora_full, 1)
                last.used(("f", 1), lora_done, 1, dn, 1)

            def expert(s, dn, n, m):
                if m == 0:
                    pe.wait_ge(lora_done, 1 * n + 1)
                last.wait(pe, ("f", m % 2))
                nc.tensor.matmul(ps_f[:, m % 2, :], wi[:, m * P:(m + 1) * P], xt[F1][:], start=True, stop=False)
                nc.tensor.matmul(ps_f[:, m % 2, :], wlb[:, m * P:(m + 1) * P], lowt[:], start=False,
                                 stop=True).then_inc(exp_full, 1)
                last.used(("f", m % 2), relued, HB, dn, m + 1)

            def down(s, dn, n, t):
                if t == 0:
                    if s == F0:
                        pe.wait_ge(gelued, 2 * n + 2)
                    else:
                        pe.wait_ge(relued, HB * n + HB)
                    last.wait(pe, ("f", 0))
                w = w3 if s == F0 else wout
                for k in range(HB):
                    done = nc.tensor.matmul(ps_f[:, 0, t * D:(t + 1) * D], hid[:, k, t * P:(t + 1) * P], w[:, k, :],
                                            start=k == 0, stop=k == HB - 1)
                if t == TILES - 1:
                    done.then_inc(out_full[s], 1)
                    last.used(("f", 0), ln[s], 5, dn, 1)

            walk(pe, dict(qkv=qkv, pass1=pass1, maxima=maxima, pass2=pass2, values=values, outputs=outputs,
                          merge=merge, project=project, turn=turn, gated=gate, hidden=hidden, route=route,
                          lora=lora, expert=expert, down=down), last)


def kernel(**inputs):
    import concourse.bacc as bacc
    from concourse.bass_utils import run_bass_kernel_spmd

    a = {k: np.asarray(t) for k, t in inputs.items()}
    x = a["L0_attn_hidden_states"].reshape(BATCH * SEQ, D)

    def by_dim(w):
        return w.reshape(*w.shape[:-1], HEADS, HD).swapaxes(-1, -2).reshape(w.shape)

    def blocks(w):
        return w.reshape(-1, P, w.shape[-1]).transpose(1, 0, 2)

    def column(w):
        return w.reshape(-1, P).T

    wqkv, bqkv = a["L1_attn_W_qkv"], a["L1_attn_b_qkv"]
    lay = {
        "x": x,
        "xt": x.T,
        "qk_a": np.stack([a["L0_attn_q_a"], a["L0_attn_k_a"]]).transpose(3, 1, 0, 2),
        "qk_b": np.stack([a["L0_attn_q_b"], a["L0_attn_k_b"]]).transpose(2, 1, 0, 3),
        "v_w0": a["L0_attn_v_w"].T,
        "o_w0": a["L0_attn_o_w"].T,
        "w12": np.stack([a["L0_ffn_w1_w"].T, a["L0_ffn_w2_w"].T], axis=1),
        "wh": np.stack([blocks(a["L0_ffn_h1_w"].T), blocks(a["L0_ffn_h2_w"].T)], axis=1),
        "w3": blocks(a["L0_ffn_w3_w"].T),
        "qk_w1": np.stack([by_dim(wqkv[:, 0:D]), by_dim(wqkv[:, D:2 * D])], axis=1),
        "v_w1": wqkv[:, 2 * D:],
        "o_w1": a["L1_attn_W_out"],
        "wi": a["L1_ffn_wi_W"].T,
        "gl": np.concatenate([a["L1_ffn_gate_W"].T, a["L1_ffn_lora_A"].reshape(ER, D).T], axis=1),
        "lb": a["L1_ffn_lora_B"].transpose(0, 2, 1).reshape(ER, HID),
        "wo": blocks(a["L1_ffn_wo_W"].T),
        "cols": np.concatenate([column(t) for t in (
            a["L0_ffn_w1_s"], a["L0_ffn_w2_s"], a["L0_ffn_h1_s"], a["L0_ffn_h2_s"], a["L1_ffn_wi_b"],
            by_dim(bqkv[0:D]), by_dim(bqkv[D:2 * D]))], axis=1),
        "rows": np.concatenate([a["L0_attn_v_b"], a["L0_attn_o_b"], a["L0_ffn_w3_s"], bqkv[2 * D:],
                                a["L1_attn_b_out"], a["L1_ffn_gate_b"], a["L1_ffn_wo_b"]]),
    }
    nc = bacc.Bacc("TRN2", target_bir_lowering=False, num_devices=1)
    arrays, aps = {}, {}
    for name, t in lay.items():
        arrays[f"in_{name}"] = np.ascontiguousarray(t)
        aps[name] = nc.dram_tensor(f"in_{name}", t.shape, F32, kind="ExternalInput").ap()
    out = nc.dram_tensor("out", (BATCH * SEQ, D), F32, kind="ExternalOutput").ap()
    build(nc, aps, out)
    got = run_bass_kernel_spmd(nc, [arrays], core_ids=[0])
    return got.results[0]["out"].reshape(BATCH, SEQ, D)
```
